# Optimizing a Trainium2 kernel written in Bass

```python
import numpy as np
import jax
import jax.numpy as jnp

def _softmax(x, axis=-1):
    return jax.nn.softmax(x, axis=axis)

def _gelu(x):
    return jax.nn.gelu(x, approximate=True)

def _silu(x):
    return jax.nn.silu(x)

def _sigmoid(x):
    return jax.nn.sigmoid(x)

def _layernorm(x, axis=-1, eps=1e-05):
    m = jnp.mean(x, axis=axis, keepdims=True)
    v = jnp.var(x, axis=axis, keepdims=True)
    return (x - m) / jnp.sqrt(v + eps)

def _scatter_add(tgt, idx, src, axis=0):
    return tgt.at[idx].add(src)

def _segment_sum(src, seg, n):
    return jax.ops.segment_sum(src, seg, n)
kernel_name = 'mk_gnn_preln_d4_gnn_r8_953ea3'

def setup_inputs(seed: int=0):
    np.random.seed(seed)
    _w = jnp.asarray

    def _rec_inputs():
        import jax
        import jax.numpy as jnp
        _gk = jax.random.key(seed)
        x = -0.0009044 + 1 * jax.random.normal(jax.random.fold_in(_gk, 1), (12500, 16), jnp.float32)
        src = jax.random.randint(jax.random.fold_in(_gk, 2), (400000,), 0, 12500, jnp.int32)
        dst = jnp.minimum((12500 * jax.random.uniform(jax.random.fold_in(_gk, 3), (400000,)) ** 2.0).astype(jnp.int32), 99999)
        _o = jnp.argsort(dst, stable=True)
        src = src[_o]
        dst = dst[_o]
        edge_attr_8 = -5.3897e-05 + 0.999841 * jax.random.normal(jax.random.fold_in(_gk, 11), (400000, 8), jnp.float32)
        node_vec1 = -0.00472126 + 0.997171 * jax.random.normal(jax.random.fold_in(_gk, 13), (12500, 1), jnp.float32)
        return (x, src, dst, edge_attr_8, node_vec1)
    x, src, dst, edge_attr_8, node_vec1 = _rec_inputs()

    def _L0_gnn_setup():
        import jax, jax.numpy as jnp
        import numpy as np
        N = 12500
        E = 100000
        F_IN = 16
        H1, C1 = (3, 32)
        H2, C2 = (1, 32)
        NC = 16
        SLOPE = 0.2

        def _gat_layer(x, src, dst, W, a_s, a_d, b, heads, outc):
            h = (x @ W).reshape(N, heads, outc)
            alpha_s = (h * a_s).sum(-1)
            alpha_d = (h * a_d).sum(-1)
            e = jax.nn.leaky_relu(alpha_s[src] + alpha_d[dst], SLOPE)
            m = jax.ops.segment_max(e, dst, num_segments=N)
            p = jnp.exp(e - m[dst])
            z = jax.ops.segment_sum(p, dst, num_segments=N)
            alpha = p / (z[dst] + 1e-16)
            out = jax.ops.segment_sum(h[src] * alpha[:, :, None], dst, num_segments=N)
            return out.reshape(N, heads * outc) + b
        key = jax.random.key(seed)
        ks = jax.random.split(key, 12)
        s = 0.1
        return {'x': jax.random.normal(ks[0], (N, F_IN), jnp.float32), 'edge_index': jax.random.randint(ks[1], (2, E), 0, N, dtype=jnp.int32), 'W1': jax.random.normal(ks[2], (F_IN, H1 * C1), jnp.float32) * s, 'a_src1': jax.random.normal(ks[3], (H1, C1), jnp.float32) * s, 'a_dst1': jax.random.normal(ks[4], (H1, C1), jnp.float32) * s, 'b1': jnp.zeros((H1 * C1,), jnp.float32), 'W2': jax.random.normal(ks[5], (H1 * C1, H2 * C2), jnp.float32) * s, 'a_src2': jax.random.normal(ks[6], (H2, C2), jnp.float32) * s, 'a_dst2': jax.random.normal(ks[7], (H2, C2), jnp.float32) * s, 'b2': jnp.zeros((H2 * C2,), jnp.float32), 'Wf': jax.random.normal(ks[8], (C2, NC), jnp.float32) * s, 'bf': jnp.zeros((NC,), jnp.float32)}
    _L0_gnn_all = _L0_gnn_setup()
    _L0_gnn_in = {k: v for k, v in _L0_gnn_all.items() if k in ('W1', 'a_src1', 'a_dst1', 'b1', 'W2', 'a_src2', 'a_dst2', 'b2', 'Wf', 'bf')}
    del _L0_gnn_all

    def _L1_gnn_setup():
        import jax, jax.numpy as jnp
        import numpy as np
        STALK_DIM = 16
        N_NODES = 6250
        N_EDGES = 50000
        HIDDEN = 64
        key = jax.random.key(seed)
        k1, k2, k3, k4 = jax.random.split(key, 4)
        d = STALK_DIM
        x = jax.random.normal(k1, (N_NODES, d), dtype=jnp.float32)
        edge_index = jax.random.randint(k2, (2, N_EDGES), 0, N_NODES, dtype=jnp.int64)
        W1 = jax.random.normal(k3, (HIDDEN, 2 * d), dtype=jnp.float32) * (1.0 / np.sqrt(2 * d))
        b1 = jnp.zeros((HIDDEN,), dtype=jnp.float32)
        W2 = jax.random.normal(k4, (d, HIDDEN), dtype=jnp.float32) * (1.0 / np.sqrt(HIDDEN))
        b2 = jnp.zeros((d,), dtype=jnp.float32)
        return {'x': x, 'edge_index': edge_index, 'W1': W1, 'b1': b1, 'W2': W2, 'b2': b2}
    _L1_gnn_all = _L1_gnn_setup()
    _L1_gnn_in = {k: v for k, v in _L1_gnn_all.items() if k in ('W1', 'b1', 'W2', 'b2')}
    del _L1_gnn_all

    def _L2_gnn_setup():
        import jax, jax.numpy as jnp
        import numpy as np
        N_NODES = 12500
        N_EDGES = 400000
        D_NODE = 16
        D_EDGE = 8
        D_HIDDEN = 16
        key = jax.random.key(seed)
        ks = jax.random.split(key, 8)
        node_features = jax.random.normal(ks[0], (N_NODES, D_NODE), dtype=jnp.float32)
        edge_attr_e3nn = jax.random.normal(ks[1], (N_EDGES, D_EDGE), dtype=jnp.float32)
        node_attr_scalar_raw = jax.random.normal(ks[2], (N_NODES, 1), dtype=jnp.float32)
        W_msg_tp = jax.random.normal(ks[3], (D_NODE, D_EDGE, D_HIDDEN), dtype=jnp.float32)
        W_msg_lin = jax.random.normal(ks[4], (D_HIDDEN, D_HIDDEN), dtype=jnp.float32)
        W_upd_tp = jax.random.normal(ks[5], (D_NODE, D_HIDDEN, D_HIDDEN), dtype=jnp.float32)
        W_upd_lin = jax.random.normal(ks[6], (D_HIDDEN, D_NODE), dtype=jnp.float32)
        edge_index = jax.random.randint(ks[7], (2, N_EDGES), 0, N_NODES, dtype=jnp.int64)
        return {'node_features': node_features, 'edge_attr_e3nn': edge_attr_e3nn, 'node_attr_scalar_raw': node_attr_scalar_raw, 'W_msg_tp': W_msg_tp, 'W_msg_lin': W_msg_lin, 'W_upd_tp': W_upd_tp, 'W_upd_lin': W_upd_lin, 'edge_index': edge_index}
    _L2_gnn_all = _L2_gnn_setup()
    _L2_gnn_in = {k: v for k, v in _L2_gnn_all.items() if k in ('W_msg_tp', 'W_msg_lin', 'W_upd_tp', 'W_upd_lin')}
    del _L2_gnn_all

    def _L3_gnn_setup():
        import jax, jax.numpy as jnp
        import numpy as np
        N_NODES = 6250
        N_EDGES = 100000
        F_IN = 16
        F_OUT = 16
        HID = 256

        def _glorot(key, shape):
            fan_in, fan_out = (shape[0], shape[1])
            lim = np.sqrt(6.0 / (fan_in + fan_out)).astype(np.float32)
            return jax.random.uniform(key, shape, jnp.float32, -lim, lim)
        key = jax.random.key(seed)
        ks = jax.random.split(key, 12)
        x = jax.random.normal(ks[0], (N_NODES, F_IN), jnp.float32)
        edge_index = jax.random.randint(ks[1], (2, N_EDGES), 0, N_NODES, jnp.int64 if jax.config.jax_enable_x64 else jnp.int32)
        return {'x': x, 'edge_index': edge_index, 'pre_w1': _glorot(ks[2], (F_IN, HID)), 'pre_b1': jnp.zeros((HID,), jnp.float32), 'pre_w2': _glorot(ks[3], (HID, HID)), 'pre_b2': jnp.zeros((HID,), jnp.float32), 'conv_w': _glorot(ks[4], (HID, HID)), 'conv_b': jnp.zeros((HID,), jnp.float32), 'post_w1': _glorot(ks[5], (2 * HID, HID)), 'post_b1': jnp.zeros((HID,), jnp.float32), 'post_w2': _glorot(ks[6], (HID, F_OUT)), 'post_b2': jnp.zeros((F_OUT,), jnp.float32)}
    _L3_gnn_all = _L3_gnn_setup()
    _L3_gnn_in = {k: v for k, v in _L3_gnn_all.items() if k in ('pre_w1', 'pre_b1', 'pre_w2', 'pre_b2', 'conv_w', 'conv_b', 'post_w1', 'post_b1', 'post_w2', 'post_b2')}
    del _L3_gnn_all
    return {'x': x, 'src': src, 'dst': dst, 'edge_attr_8': edge_attr_8, 'node_vec1': node_vec1, 'L0_gnn_W1': _L0_gnn_in['W1'], 'L0_gnn_a_src1': _L0_gnn_in['a_src1'], 'L0_gnn_a_dst1': _L0_gnn_in['a_dst1'], 'L0_gnn_b1': _L0_gnn_in['b1'], 'L0_gnn_W2': _L0_gnn_in['W2'], 'L0_gnn_a_src2': _L0_gnn_in['a_src2'], 'L0_gnn_a_dst2': _L0_gnn_in['a_dst2'], 'L0_gnn_b2': _L0_gnn_in['b2'], 'L0_gnn_Wf': _L0_gnn_in['Wf'], 'L0_gnn_bf': _L0_gnn_in['bf'], 'L1_gnn_W1': _L1_gnn_in['W1'], 'L1_gnn_b1': _L1_gnn_in['b1'], 'L1_gnn_W2': _L1_gnn_in['W2'], 'L1_gnn_b2': _L1_gnn_in['b2'], 'L2_gnn_W_msg_tp': _L2_gnn_in['W_msg_tp'], 'L2_gnn_W_msg_lin': _L2_gnn_in['W_msg_lin'], 'L2_gnn_W_upd_tp': _L2_gnn_in['W_upd_tp'], 'L2_gnn_W_upd_lin': _L2_gnn_in['W_upd_lin'], 'L3_gnn_pre_w1': _L3_gnn_in['pre_w1'], 'L3_gnn_pre_b1': _L3_gnn_in['pre_b1'], 'L3_gnn_pre_w2': _L3_gnn_in['pre_w2'], 'L3_gnn_pre_b2': _L3_gnn_in['pre_b2'], 'L3_gnn_conv_w': _L3_gnn_in['conv_w'], 'L3_gnn_conv_b': _L3_gnn_in['conv_b'], 'L3_gnn_post_w1': _L3_gnn_in['post_w1'], 'L3_gnn_post_b1': _L3_gnn_in['post_b1'], 'L3_gnn_post_w2': _L3_gnn_in['post_w2'], 'L3_gnn_post_b2': _L3_gnn_in['post_b2']}

def reference(x, src, dst, edge_attr_8, node_vec1, L0_gnn_W1, L0_gnn_a_src1, L0_gnn_a_dst1, L0_gnn_b1, L0_gnn_W2, L0_gnn_a_src2, L0_gnn_a_dst2, L0_gnn_b2, L0_gnn_Wf, L0_gnn_bf, L1_gnn_W1, L1_gnn_b1, L1_gnn_W2, L1_gnn_b2, L2_gnn_W_msg_tp, L2_gnn_W_msg_lin, L2_gnn_W_upd_tp, L2_gnn_W_upd_lin, L3_gnn_pre_w1, L3_gnn_pre_b1, L3_gnn_pre_w2, L3_gnn_pre_b2, L3_gnn_conv_w, L3_gnn_conv_b, L3_gnn_post_w1, L3_gnn_post_b1, L3_gnn_post_w2, L3_gnn_post_b2):
    import jax
    import jax.numpy as jnp

    def _L0_gnn_ref(x, edge_index, W1, a_src1, a_dst1, b1, W2, a_src2, a_dst2, b2, Wf, bf):
        import jax, jax.numpy as jnp
        import numpy as np
        N = 12500
        E = 100000
        F_IN = 16
        H1, C1 = (3, 32)
        H2, C2 = (1, 32)
        NC = 16
        SLOPE = 0.2

        def _gat_layer(x, src, dst, W, a_s, a_d, b, heads, outc):
            h = (x @ W).reshape(N, heads, outc)
            alpha_s = (h * a_s).sum(-1)
            alpha_d = (h * a_d).sum(-1)
            e = jax.nn.leaky_relu(alpha_s[src] + alpha_d[dst], SLOPE)
            m = jax.ops.segment_max(e, dst, num_segments=N)
            p = jnp.exp(e - m[dst])
            z = jax.ops.segment_sum(p, dst, num_segments=N)
            alpha = p / (z[dst] + 1e-16)
            out = jax.ops.segment_sum(h[src] * alpha[:, :, None], dst, num_segments=N)
            return out.reshape(N, heads * outc) + b
        loops = jnp.arange(N, dtype=edge_index.dtype)
        src = jnp.concatenate([edge_index[0], loops])
        dst = jnp.concatenate([edge_index[1], loops])
        h = jax.nn.selu(_gat_layer(x, src, dst, W1, a_src1, a_dst1, b1, H1, C1))
        h = jax.nn.selu(_gat_layer(h, src, dst, W2, a_src2, a_dst2, b2, H2, C2))
        return h @ Wf + bf

    def _L1_gnn_ref(x, edge_index, W1, b1, W2, b2):
        import jax, jax.numpy as jnp
        import numpy as np
        STALK_DIM = 16
        N_NODES = 6250
        N_EDGES = 50000
        HIDDEN = 64
        d = x.shape[1]
        n = x.shape[0]
        src, dst = (edge_index[0], edge_index[1])
        xs, xd = (x[src], x[dst])

        def reflection(a, b):
            h = jax.nn.relu(jnp.concatenate([a, b], axis=1) @ W1.T + b1)
            return h @ W2.T + b2

        def householder(v):
            vn = v / jnp.maximum(jnp.linalg.norm(v, axis=1, keepdims=True), 1e-12)
            return jnp.eye(d, dtype=v.dtype)[None] - 2.0 * vn[:, :, None] * vn[:, None, :]
        F_s = householder(reflection(xs, xd))
        F_d = householder(reflection(xd, xs))
        L_sd = -jnp.einsum('eki,ekj->eij', F_s, F_d)
        ones_e = jnp.ones(src.shape[0], dtype=x.dtype)
        deg = jnp.zeros(n, dtype=x.dtype).at[src].add(ones_e).at[dst].add(ones_e)
        deg_inv_sqrt = 1.0 / jnp.sqrt(jnp.maximum(deg, 1e-05))
        coef = deg_inv_sqrt[src] * deg_inv_sqrt[dst]
        msg_s = coef[:, None] * jnp.einsum('eij,ej->ei', L_sd, xd)
        msg_d = coef[:, None] * jnp.einsum('eji,ej->ei', L_sd, xs)
        out = x - jnp.zeros_like(x).at[src].add(msg_s) - jnp.zeros_like(x).at[dst].add(msg_d)
        return jax.nn.relu(out)

    def _L2_gnn_ref(node_features, edge_attr_e3nn, node_attr_scalar_raw, W_msg_tp, W_msg_lin, W_upd_tp, W_upd_lin, edge_index):
        import jax, jax.numpy as jnp
        import numpy as np
        N_NODES = 12500
        N_EDGES = 400000
        D_NODE = 16
        D_EDGE = 8
        D_HIDDEN = 16
        n_nodes = node_features.shape[0]
        row = edge_index[0]
        col = edge_index[1]
        norm_msg_tp = 1.0 / np.float32(np.sqrt(D_NODE * D_EDGE))
        norm_upd_tp = 1.0 / np.float32(np.sqrt(D_NODE * D_HIDDEN))
        norm_lin = 1.0 / np.float32(np.sqrt(D_HIDDEN))
        x_j = node_features[col]
        m = jnp.einsum('ei,ej,ijh->eh', x_j, edge_attr_e3nn, W_msg_tp) * norm_msg_tp
        m = jax.nn.silu(m)
        m = m @ W_msg_lin * norm_lin
        agg = jax.ops.segment_sum(m, row, num_segments=n_nodes)
        u = jnp.einsum('ni,nh,ihk->nk', node_features, agg, W_upd_tp) * norm_upd_tp
        u = jax.nn.silu(u)
        u = u @ W_upd_lin * norm_lin
        return node_features + u

    def _L3_gnn_ref(x, edge_index, pre_w1, pre_b1, pre_w2, pre_b2, conv_w, conv_b, post_w1, post_b1, post_w2, post_b2):
        import jax, jax.numpy as jnp
        import numpy as np
        N_NODES = 6250
        N_EDGES = 100000
        F_IN = 16
        F_OUT = 16
        HID = 256

        def _glorot(key, shape):
            fan_in, fan_out = (shape[0], shape[1])
            lim = np.sqrt(6.0 / (fan_in + fan_out)).astype(np.float32)
            return jax.random.uniform(key, shape, jnp.float32, -lim, lim)
        h = jax.nn.relu(x @ pre_w1 + pre_b1) @ pre_w2 + pre_b2
        src, dst = (edge_index[0], edge_index[1])
        msg = jax.nn.relu(h[src] @ conv_w + conv_b)
        agg = jax.ops.segment_sum(msg, dst, num_segments=h.shape[0])
        h = jnp.concatenate([h, agg], axis=-1)
        out = jax.nn.relu(h @ post_w1 + post_b1) @ post_w2 + post_b2
        return jnp.tanh(out)
    edge_index = jnp.stack([src, dst])
    h = jnp.maximum(_layernorm(x, axis=-1), 0.0)
    x = x + _L0_gnn_ref(h, edge_index, L0_gnn_W1, L0_gnn_a_src1, L0_gnn_a_dst1, L0_gnn_b1, L0_gnn_W2, L0_gnn_a_src2, L0_gnn_a_dst2, L0_gnn_b2, L0_gnn_Wf, L0_gnn_bf)
    h = jnp.maximum(_layernorm(x, axis=-1), 0.0)
    x = x + _L1_gnn_ref(h, edge_index, L1_gnn_W1, L1_gnn_b1, L1_gnn_W2, L1_gnn_b2)
    h = jnp.maximum(_layernorm(x, axis=-1), 0.0)
    x = x + _L2_gnn_ref(h, edge_attr_8, node_vec1, L2_gnn_W_msg_tp, L2_gnn_W_msg_lin, L2_gnn_W_upd_tp, L2_gnn_W_upd_lin, edge_index)
    h = jnp.maximum(_layernorm(x, axis=-1), 0.0)
    x = x + _L3_gnn_ref(h, edge_index, L3_gnn_pre_w1, L3_gnn_pre_b1, L3_gnn_pre_w2, L3_gnn_pre_b2, L3_gnn_conv_w, L3_gnn_conv_b, L3_gnn_post_w1, L3_gnn_post_b1, L3_gnn_post_w2, L3_gnn_post_b2)
    return x

_drawn_inputs = setup_inputs


def setup_inputs(seed=0):
    import zlib

    import numpy as np

    out = dict(_drawn_inputs(seed))
    spreads = {'L0_gnn_b1': (0.0, 0.1),
     'L0_gnn_b2': (0.0, 0.1),
     'L0_gnn_bf': (0.0, 0.1),
     'L1_gnn_b1': (0.0, 0.742),
     'L1_gnn_b2': (0.0, 0.632),
     'L3_gnn_pre_b1': (0.0, 0.1),
     'L3_gnn_pre_b2': (0.0, 0.1),
     'L3_gnn_conv_b': (0.0, 0.1),
     'L3_gnn_post_b1': (0.0, 0.8),
     'L3_gnn_post_b2': (0.0, 0.608)}
    factors = {'L0_gnn_a_src1': 8.0,
     'L0_gnn_a_dst1': 35.373,
     'L0_gnn_a_src2': 64.0,
     'L0_gnn_a_dst2': 200.0}
    for name, (base, spread) in spreads.items():
        noise = np.random.default_rng([zlib.crc32(name.encode()), seed]).standard_normal(out[name].shape)
        drawn = base * np.exp(spread * noise) if base else spread * noise
        out[name] = jnp.asarray(drawn.astype(out[name].dtype))
    for name, factor in factors.items():
        out[name] = (out[name] * factor).astype(out[name].dtype)
    return out
```

```python
from contextlib import ExitStack

import concourse.bass as bass
from concourse import mybir

F32 = mybir.dt.float32
I32 = mybir.dt.int32
BF16 = mybir.dt.bfloat16
ALU = mybir.AluOpType
ACT = mybir.ActivationFunctionType
AX = mybir.AxisListType
ds = bass.ds

P = 128
N = 12500
E = 400000
D = 16
EP = E // P
NT = -(-N // P)
NP = NT * P
CH = 125
NCH = EP // CH
SUB = 25
FULL = N // NT
REST = N - FULL * NT
BIG = 1e30
HID = 256
SETS = 2
PER_SET = 5
assert EP * P == E and NCH * CH == EP


def bcast(ap, shape):
    return ap.to_broadcast(shape)


class Chain:

    def __init__(self, eng, sem, base=0):
        self.eng, self.sem, self.base, self.n = eng, sem, base, 0

    def __call__(self, ins):
        ins.then_inc(self.sem, 1)
        self.n += 1
        self.eng.wait_ge(self.sem, self.base + self.n)


def chunks(eng, count, peel, body, ring=2, tail=0):
    assert (count - peel - tail) % ring == 0
    for k in range(peel):
        body(k, k % ring)
    with eng.Fori(0, (count - peel - tail) // ring) as i:
        for j in range(ring):
            body(i * ring + (peel + j), (peel + j) % ring)
    for k in range(count - tail, count):
        body(k, k % ring)


def held(eng, *values):
    return [v if isinstance(v, int) else eng.snap(v) for v in values]


def first(k, n):
    return isinstance(k, int) and k < n


class Kernel:
    def __init__(self, nc, ctx, t, out):
        self.nc, self.ctx, self.t, self.out = nc, ctx, t, out
        self.uid = 0
        self.sem_seen, self.sem_old = set(), []

    def sb(self, name, shape, dt=F32, ctx=None):
        self.uid += 1
        return (ctx or self.ctx).enter_context(self.nc.sbuf_tensor(f"{name}_{self.uid}", shape, dt))

    def ps(self, name, shape, ctx):
        self.uid += 1
        return ctx.enter_context(self.nc.psum_tensor(f"{name}_{self.uid}", shape, F32))

    def sem(self, name, ctx):
        self.uid += 1
        s = ctx.enter_context(self.nc.semaphore(f"{name}_{self.uid}"))
        if s.num in self.sem_seen:
            self.sem_old.append(s)
        self.sem_seen.add(s.num)
        return s

    def dsem(self, name):
        return self.sem(name, self.ctx)

    def block(self):
        if self.sem_old:
            for s in self.sem_old:
                self.nc.sync.sem_clear(s)
            self.sem_old = []
            self.nc.all_engine_barrier()
        return self.nc.Block()

    def dram(self, name, shape, dt=F32):
        return self.nc.dram_tensor(name, shape, dt, kind="Internal").ap()

    def setup(self):
        nc, t = self.nc, self.t
        sb = self.sb
        self.ident = sb("ident", [P, P])
        self.lower = sb("lower", [P, P])
        self.same = sb("same", [P, EP])
        self.srcf = sb("srcf", [P, EP])
        self.sidx = sb("sidx", [P, EP], I32)
        self.X = sb("X", [P, NT, D])
        self.H = sb("H", [P, NT, D])
        self.end_i = sb("end_i", [P, NT], I32)
        self.start_i = sb("start_i", [P, NT], I32)
        self.deg_d = sb("deg_d", [P, NT])
        self.deg_s = sb("deg_s", [P, NT])
        self.dst0_i = sb("dst0_i", [P, 1], I32)
        self.fe_i = sb("fe_i", [P, 1], I32)
        self.cont = sb("cont", [P, P])
        self.flag = sb("flag", [P, P])
        self.trash = sb("trash", [P, 1])
        self.tail = sb("last_rows", [P, HID])
        self.starts3 = self.dram("starts3", (E + NP, 3))
        self.starts1 = self.dram("starts1", (E + NP, 1))
        self.starts17 = self.dram("starts17", (E + NP, D + 1))
        self.acc = [self.dram(f"acc{i}", (NP + P, D)) for i in range(SETS * PER_SET)]

        with ExitStack() as c:
            dsti = sb("dsti", [P, EP], I32, c)
            dstf = sb("dstf", [P, EP], F32, c)
            io = sb("iota_node", [P, NT + 1], F32, c)
            ioi = sb("iota_node_i", [P, NT + 1], I32, c)
            pi = sb("iota_part_i", [P, 1], I32, c)
            pf = sb("iota_part", [P, 1], F32, c)
            zer = sb("zeros", [P, 2048], F32, c)
            s_in, s_dve, s_pool, s_pe = (self.sem(x, c) for x in ("loaded", "dve_done", "pool_done", "pe_done"))
            s_z, s_x, s_samp, s_prep = (self.sem(x, c) for x in ("zeroed", "x_loaded", "samples_written", "prepared"))
            pq = self.ps("bc", [P, 512], c)
            NB = EP // SUB
            samp = sb("samp", [P, NB], F32, c)
            samples = self.dram("samples", (P, NB))
            with self.block() as block:
                @block.sync
                def _(sp):
                    sp.dma_start(dsti[:], t["dst"].rearrange("(p c) -> p c", p=P)).then_inc(s_in, 16)
                    sp.dma_start(self.sidx[:], t["src"].rearrange("(p c) -> p c", p=P)).then_inc(s_in, 16)
                    sp.wait_ge(s_dve, 2)
                    sp.dma_start(self.X[0:FULL, :, :], t["x"][0:FULL * NT, :].rearrange("(p t) d -> p t d", t=NT)).then_inc(s_x, 16)
                    sp.dma_start(self.X[FULL:FULL + 1, 0:REST, :], t["x"][FULL * NT:N, :].rearrange("(p t) d -> p t d", p=1)).then_inc(s_x, 16)
                    sp.wait_ge(s_dve, 4)
                    sp.dma_start(samples, samp[:]).then_inc(s_samp, 16)
                    n = 0
                    for tab, w in ((self.starts3, 3), (self.starts1, 1), (self.starts17, D + 1)):
                        flat = tab[0:E, :].rearrange("(p c) w -> p (c w)", p=P)
                        tot = EP * w
                        step = 2048
                        whole = tot // step
                        if whole:
                            sp.dma_start(flat[:, 0:whole * step].rearrange("p (r s) -> p r s", s=step),
                                         bcast(zer[:].unsqueeze(1), [P, whole, step])).then_inc(s_z, 16)
                            n += 1
                        if tot % step:
                            sp.dma_start(flat[:, whole * step:tot], zer[:, 0:tot % step]).then_inc(s_z, 16)
                            n += 1
                    for a in self.acc:
                        sp.dma_start(a.rearrange("(p c) w -> p (c w)", p=P), zer[:, 0:(NP + P) * D // P]).then_inc(s_z, 16)
                        n += 1
                    self.cleared = 16 * n
                    sp.wait_ge(s_x, 32)
                    sp.wait_ge(s_samp, 16)

                @block.gpsimd
                def _(g):
                    g.memset(self.ident[:], 0.0).then_inc(s_pool, 1)
                    g.memset(self.lower[:], 1.0).then_inc(s_pool, 1)
                    g.iota(ioi[:], pattern=[[1, NT + 1]], base=0, channel_multiplier=NT).then_inc(s_pool, 1)
                    g.iota(pi[:], pattern=[[0, 1]], base=0, channel_multiplier=1).then_inc(s_pool, 1)
                    g.wait_ge(s_pool, 4)
                    g.affine_select(out=self.ident[:], in_=self.ident[:], compare_op=ALU.not_equal, fill=1.0,
                                    base=0, pattern=[[-1, P]], channel_multiplier=1).then_inc(s_pool, 1)
                    g.affine_select(out=self.lower[:], in_=self.lower[:], compare_op=ALU.is_gt, fill=0.0,
                                    base=0, pattern=[[-1, P]], channel_multiplier=1).then_inc(s_pool, 1)

                @block.vector
                def _(v):
                    v.memset(self.X[:], 0.0).then_inc(s_dve, 1)
                    v.memset(zer[:], 0.0).then_inc(s_dve, 1)
                    v.wait_ge(s_in, 32)
                    v.tensor_copy(dstf[:], dsti[:]).then_inc(s_dve, 1)
                    v.wait_ge(s_dve, 3)
                    v.tensor_copy(samp[:], dstf[:, 0:EP:SUB]).then_inc(s_dve, 1)
                    v.tensor_copy(self.srcf[:], self.sidx[:])
                    v.tensor_copy(self.dst0_i[:], dsti[:, 0:1])
                    v.memset(self.same[:, 0:1], 0.0)
                    v.tensor_tensor(self.same[:, 1:EP], dstf[:, 1:EP], dstf[:, 0:EP - 1], ALU.is_equal)
                    v.wait_ge(s_pool, 4)
                    v.tensor_copy(io[:], ioi[:])
                    v.tensor_copy(pf[:], pi[:]).then_inc(s_dve, 1)

                @block.tensor
                def _(pe):
                    pe.wait_ge(s_pool, 6)
                    pe.wait_ge(s_dve, 3)
                    pe.matmul(pq[:, 0:P], bcast(dstf[:, 0:1], [P, P]), self.ident[:], start=True, stop=True)
                    pe.matmul(pq[:, P:2 * P], bcast(dstf[:, EP - 1:EP], [P, P]), self.ident[:], start=True, stop=True).then_inc(s_pe, 1)

            row0 = sb("row0", [P, P], F32, c)
            rowl = sb("rowl", [P, P], F32, c)
            q3 = (NT + 1) // 3
            cmp_ = sb("cmp", [P, q3, P], F32, c)
            part = sb("part", [P, NT + 1], F32, c)
            blk_ = sb("blk", [P, NT + 1], F32, c)
            rp = sb("rowptr", [P, NT + 1], F32, c)
            idx = sb("idx", [P, NT + 1], I32, c)
            idx2 = sb("idx2", [P, NT + 1], I32, c)
            g2 = sb("g2", [P, q3, NB], F32, c)
            g3 = sb("g3", [P, NT + 1, SUB], I32, c)
            tmp = sb("tmp", [P, NT], F32, c)
            pos = sb("pos", [P, NT], F32, c)
            s_v, s_i, s_g2u = (self.sem(x, c) for x in ("dve_chain", "indices", "samples_used"))
            s_g2, s_g3 = self.dsem("samples_in"), self.dsem("edges_in")
            with self.block() as block:
                @block.vector
                def _(v):
                    w = Chain(v, s_v)
                    v.tensor_copy(row0[:], pq[:, 0:P])
                    w(v.tensor_copy(rowl[:], pq[:, P:2 * P]))
                    v.memset(self.cont[:, 0:1], 0.0)
                    w(v.tensor_tensor(self.cont[:, 1:P], row0[:, 1:P], rowl[:, 0:P - 1], ALU.is_equal))
                    w(v.tensor_tensor(self.flag[:], row0[:], rowl[:], ALU.is_equal))
                    w(v.tensor_tensor(self.flag[:], self.flag[:], self.cont[:], ALU.mult))
                    w(v.tensor_tensor(dsti[:].bitcast(F32), dstf[:], bcast(dstf[:, 0:1], [P, EP]), ALU.is_equal))
                    w(v.tensor_reduce(tmp[:, 0:1], dsti[:].bitcast(F32), AX.X, ALU.add))
                    w(v.tensor_scalar(tmp[:, 1:2], pf[:], float(EP), -1.0, ALU.mult, ALU.add))
                    w(v.tensor_tensor(self.fe_i[:], tmp[:, 0:1], tmp[:, 1:2], ALU.add))
                    w(v.tensor_scalar(self.trash[:], pf[:], float(NP), None, ALU.add))
                    for s in range(3):
                        a = s * q3
                        w(v.tensor_tensor(cmp_[:], bcast(row0[:].unsqueeze(1), [P, q3, P]),
                                          bcast(io[:, a:a + q3].unsqueeze(2), [P, q3, P]), ALU.is_lt))
                        w(v.tensor_reduce(part[:, a:a + q3], cmp_[:], AX.X, ALU.add))
                    w(v.tensor_scalar(part[:], part[:], -1.0, 0.0, ALU.add, ALU.max))
                    v.tensor_copy(idx[:], part[:]).then_inc(s_i, 1)
                    for s in range(3):
                        a = s * q3
                        v.wait_ge(s_g2, 16 * q3 * (s + 1))
                        w(v.tensor_tensor(cmp_[:, :, 0:NB], g2[:], bcast(io[:, a:a + q3].unsqueeze(2), [P, q3, NB]), ALU.is_lt))
                        w(v.tensor_reduce(blk_[:, a:a + q3], cmp_[:, :, 0:NB], AX.X, ALU.add))
                        v.sem_inc(s_g2u, 1)
                    w(v.tensor_scalar(blk_[:], blk_[:], -1.0, 0.0, ALU.add, ALU.max))
                    w(v.scalar_tensor_tensor(blk_[:], part[:], float(NB), blk_[:], ALU.mult, ALU.add))
                    v.tensor_copy(idx2[:], blk_[:]).then_inc(s_i, 1)
                    v.wait_ge(s_g3, 16 * (NT + 1))
                    g3f = cmp_[:].rearrange("p a b -> p (a b)")[:, 0:(NT + 1) * SUB].rearrange("p (a b) -> p a b", b=SUB)
                    w(v.tensor_tensor(g3f, g3[:], bcast(io[:].unsqueeze(2), [P, NT + 1, SUB]), ALU.is_lt))
                    w(v.tensor_reduce(rp[:], g3f, AX.X, ALU.add))
                    w(v.scalar_tensor_tensor(rp[:], blk_[:], float(SUB), rp[:], ALU.mult, ALU.add))
                    w(v.tensor_tensor(self.deg_d[:], rp[:, 1:NT + 1], rp[:, 0:NT], ALU.subtract))
                    w(v.tensor_scalar(pos[:], self.deg_d[:], 0.5, None, ALU.is_gt))
                    w(v.tensor_scalar(tmp[:], rp[:, 1:NT + 1], float(-1 - E), None, ALU.add))
                    w(v.tensor_tensor(tmp[:], tmp[:], pos[:], ALU.mult))
                    w(v.tensor_scalar(self.end_i[:], tmp[:], float(E), None, ALU.add))
                    w(v.tensor_scalar(io[:], io[:], float(E), None, ALU.add))
                    w(v.tensor_tensor(tmp[:], rp[:, 0:NT], io[:, 0:NT], ALU.subtract))
                    w(v.tensor_tensor(tmp[:], tmp[:], pos[:], ALU.mult))
                    w(v.tensor_tensor(self.start_i[:], tmp[:], io[:, 0:NT], ALU.add))

                @block.gpsimd
                def _(g):
                    g.wait_ge(s_i, 1)
                    for s in range(3):
                        if s:
                            g.wait_ge(s_g2u, s)
                        for a in range(q3):
                            g.indirect_dma_start(g2[:, a, :], None, samples, bass.IndirectOffsetOnAxis(
                                ap=idx[:, s * q3 + a:s * q3 + a + 1], axis=0)).then_inc(s_g2, 16)
                    g.wait_ge(s_z, self.cleared)
                    g.wait_ge(s_i, 2)
                    rows = t["dst"].rearrange("(r c) -> r c", c=SUB)
                    for a in range(NT + 1):
                        g.indirect_dma_start(g3[:, a, :], None, rows, bass.IndirectOffsetOnAxis(
                            ap=idx2[:, a:a + 1], axis=0)).then_inc(s_g3, 16)

    def layer_norm(self):
        nc = self.nc
        with ExitStack() as c:
            m = self.sb("mean", [P, NT], F32, c)
            q = self.sb("square", [P, NT, D], F32, c)
            s = self.sb("std", [P, NT], F32, c)
            r2 = self.sb("newton", [P, NT], F32, c)
            eps = self.sb("eps", [P, 1], F32, c)
            s_v, s_var, s_std = (self.sem(x, c) for x in ("dve_chain", "variance", "std"))
            with self.block() as block:
                @block.vector
                def _(v):
                    w = Chain(v, s_v)
                    v.memset(eps[:], 1e-5)
                    w(v.tensor_reduce(m[:], self.X[:], AX.X, ALU.add))
                    w(v.tensor_scalar(m[:], m[:], 1.0 / D, None, ALU.mult))
                    w(v.tensor_tensor(self.H[:], self.X[:], bcast(m[:].unsqueeze(2), [P, NT, D]), ALU.subtract))
                    w(v.tensor_tensor(q[:], self.H[:], self.H[:], ALU.mult))
                    w(v.tensor_reduce(s[:], q[:], AX.X, ALU.add))
                    v.tensor_scalar(s[:], s[:], 1.0 / D, None, ALU.mult).then_inc(s_var, 1)
                    v.wait_ge(s_std, 1)
                    w(v.reciprocal(m[:], m[:]))
                    w(v.tensor_tensor(r2[:], m[:], m[:], ALU.mult))
                    w(v.scalar_tensor_tensor(r2[:], s[:], 1e-5, r2[:], ALU.add, ALU.mult))
                    w(v.tensor_scalar(r2[:], r2[:], -0.5, 1.5, ALU.mult, ALU.add))
                    w(v.tensor_tensor(m[:], m[:], r2[:], ALU.mult))
                    w(v.tensor_tensor(self.H[:], self.H[:], bcast(m[:].unsqueeze(2), [P, NT, D]), ALU.mult))
                    v.tensor_scalar(self.H[:], self.H[:], 0.0, None, ALU.max).then_inc(s_var, 1)

                @block.scalar
                def _(a):
                    a.wait_ge(s_var, 1)
                    nc.scalar.activation(m[:], s[:], ACT.Sqrt, bias=eps[:]).then_inc(s_std, 1)

    def linear(self, X, K, W, M, Y, bias=None, add=False):
        nc = self.nc
        GT = 7 if M <= 36 else 2
        groups = NT // GT
        assert groups * GT == NT
        with ExitStack() as c:
            pt = [self.ps(f"xT_ps{b}", [P, 2, 512], c) for b in range(2)]
            py = [self.ps(f"y_ps{b}", [P, 512], c) for b in range(2)]
            xT = [self.sb(f"xT{b}", [P, GT * P], F32, c) for b in range(2)]
            xs = [self.sb(f"staged{b}", [P, GT, K], F32, c) for b in range(2)]
            s_s, s_p = self.sem("staged", c), self.sem("pe_passed", c)
            s_t, s_c, s_y, s_o = (self.sem(x, c) for x in ("transposed", "copied", "product", "stored"))
            at = lambda b, i: pt[b][0:K, i // 4, (i % 4) * P:(i % 4 + 1) * P]
            loop = dict(peel=2, tail=2 - groups % 2)
            with self.block() as block:
                @block.gpsimd
                def _(pool):
                    def stage(g, b):
                        if not first(g, 2):
                            pool.wait_ge(s_t, g - 1)
                        pool.tensor_copy(xs[b][:], X[:, ds(g * GT, GT), 0:K]).then_inc(s_s, 1)
                    chunks(pool, groups, body=stage, **loop)

                @block.tensor
                def _(pe):
                    def turn(g, b):
                        pe.wait_ge(s_s, g + 1)
                        pe.sem_inc(s_p, 1)
                        if not first(g, 2):
                            pe.wait_ge(s_c, g - 1)
                            pe.sem_inc(s_p, 1)
                        for i in range(GT):
                            last = pe.transpose(at(b, i), xs[b][:, i, :], self.ident[:])
                        last.then_inc(s_t, 1)

                    def product(g, b):
                        if not (isinstance(g, int) and g == groups - 1):
                            turn(g + 1, 1 - b)
                        pe.wait_ge(s_c, g + 1)
                        if not first(g, 2):
                            pe.wait_ge(s_o, g - 1)
                        for i in range(GT):
                            last = pe.matmul(py[b][:, i * M:(i + 1) * M], xT[b][0:K, i * P:(i + 1) * P], W, start=True, stop=True)
                        last.then_inc(s_y, 1)
                    turn(0, 0)
                    chunks(pe, groups, body=product, **loop)

                @block.scalar
                def _(a):
                    def copy(g, b):
                        a.wait_ge(s_t, g + 1)
                        if not first(g, 2):
                            a.wait_ge(s_y, g - 1)
                        n4 = min(GT, 4)
                        last = nc.scalar.activation(xT[b][0:K, 0:n4 * P], pt[b][0:K, 0, 0:n4 * P], ACT.Copy)
                        if GT > 4:
                            last = nc.scalar.activation(xT[b][0:K, 4 * P:GT * P], pt[b][0:K, 1, 0:(GT - 4) * P], ACT.Copy)
                        last.then_inc(s_c, 1)
                    chunks(a, groups, body=copy, **loop)

                @block.vector
                def _(v):
                    def store(g, b):
                        y = Y[:, ds(g * GT, GT), 0:M]
                        src = py[b][:, 0:GT * M].rearrange("p (a m) -> p a m", m=M)
                        v.wait_ge(s_y, g + 1)
                        if bias is not None:
                            v.tensor_tensor(y, src, bcast(bias.unsqueeze(1), [P, GT, M]), ALU.add).then_inc(s_o, 1)
                        elif add:
                            v.tensor_tensor(y, src, y, ALU.add).then_inc(s_o, 1)
                        else:
                            v.tensor_scalar(y, src, 0.0, None, ALU.add).then_inc(s_o, 1)
                    chunks(v, groups, body=store, **loop)

    def table(self, T, width, tab, starts=None, col=0, w=0):
        nc = self.nc
        with ExitStack() as c:
            s_t = self.sem("table_written", c)
            s_s = self.dsem("starts_written") if starts is not None else None
            with self.block() as block:
                @block.sync
                def _(sp):
                    sp.dma_start(tab.rearrange("(p t) w -> p t w", p=P), T[:, :, 0:width]).then_inc(s_t, 16)
                    sp.wait_ge(s_t, 16)

                @block.gpsimd
                def _(g):
                    if starts is None:
                        return
                    for i in range(NT):
                        g.indirect_dma_start(starts, bass.IndirectOffsetOnAxis(ap=self.start_i[:, i:i + 1], axis=0),
                                             T[:, i, col:col + w], None).then_inc(s_s, 16)
                    g.wait_ge(s_s, 16 * NT)

    def fixup(self, rows, W, tail, heads=0):
        nc = self.nc
        R = W + heads
        pieces = [(a, min(P, W - a)) for a in range(0, W, P)]
        with ExitStack() as c:
            sb, ps, sem = (lambda n, s, d=F32: self.sb(n, s, d, c)), (lambda n, s: self.ps(n, s, c)), (lambda n: self.sem(n, c))
            got = sb("first_run_rows", [P, R])
            mx = sb("tail_max", [P, W])
            mxr = sb("row_max", [P, W])
            S = sb("sums", [P, 1 + P])
            M = sb("maxima", [P, 1 + P])
            T = sb("scratch", [P, P])
            U = sb("scratch2", [P, P])
            neg = sb("neg", [P, P])
            nc_ = sb("neg_cont", [P, P])
            neutral = sb("neutral", [1, R])
            A = ps("transposed", [P, 4, P])
            B = ps("back", [P, 4, P])
            s_v, s_pe, s_vp, s_act, s_va = (sem(x) for x in (
                "dve_chain", "pe_done", "dve_for_pe", "exp_done", "dve_for_act"))
            s_g, s_out = self.dsem("rows_in"), self.dsem("rows_out")
            s_n = sem("neutral_out")
            off = bass.IndirectOffsetOnAxis(ap=self.fe_i[:], axis=0)
            with self.block() as block:
                @block.gpsimd
                def _(g):
                    g.wait_ge(s_n, 16)
                    g.indirect_dma_start(got[:], None, rows, off).then_inc(s_g, 16)
                    g.wait_ge(s_vp, 2 * len(pieces) + 1)
                    g.indirect_dma_start(rows, off, got[:], None).then_inc(s_out, 16)
                    g.wait_ge(s_out, 16)

                @block.sync
                def _(sp):
                    sp.wait_ge(s_vp, 1)
                    sp.dma_start(rows[E:E + 1, :], neutral[:]).then_inc(s_n, 16)
                    sp.wait_ge(s_n, 16)

                @block.tensor
                def _(pe):
                    for n, (a, m) in enumerate(pieces):
                        pe.wait_ge(s_vp, 2 * n + 1)
                        last = pe.transpose(A[0:m, 0, :], tail[:, a:a + m], self.ident[:])
                        if heads:
                            last = pe.transpose(A[0:m, 1, :], mx[:, 0:m], self.ident[:])
                        last.then_inc(s_pe, 1)
                        pe.wait_ge(s_vp, 2 * n + 2)
                        last = pe.transpose(B[:, 0, 0:m], S[0:m, 1:1 + P], self.ident[0:m, 0:m])
                        if heads:
                            last = pe.transpose(B[:, 1, 0:m], M[0:m, 1:1 + P], self.ident[0:m, 0:m])
                        last.then_inc(s_pe, 1)

                @block.scalar
                def _(act):
                    if heads:
                        act.wait_ge(s_va, 1)
                        nc.scalar.activation(T[0:W, :], T[0:W, :], ACT.Exp)
                        nc.scalar.activation(U[0:W, :], U[0:W, :], ACT.Exp).then_inc(s_act, 1)
                        act.wait_ge(s_va, 2)
                        nc.scalar.activation(T[:, 0:W], T[:, 0:W], ACT.Exp)
                        nc.scalar.activation(U[:, 0:W], U[:, 0:W], ACT.Exp).then_inc(s_act, 1)

                @block.vector
                def _(v):
                    w = Chain(v, s_v)
                    F = W // max(heads, 1)
                    heads_of = lambda ap: ap.rearrange("p (h f) -> p h f", h=heads)
                    w(v.memset(neutral[:], 0.0))
                    if heads:
                        v.memset(neutral[:, W:R], -BIG)
                        v.tensor_scalar(neg[:], self.flag[:], 1.0, BIG, ALU.subtract, ALU.mult)
                        v.tensor_scalar(nc_[:], self.cont[:], 1.0, BIG, ALU.subtract, ALU.mult)
                        w(v.tensor_copy(heads_of(mx[:]), bcast(tail[:, W:R].unsqueeze(2), [P, heads, F])))
                    v.memset(M[:, 0:1], -BIG)
                    v.memset(S[:, 0:1], 0.0).then_inc(s_vp, 1)
                    for n, (a, m) in enumerate(pieces):
                        v.wait_ge(s_pe, 2 * n + 1)
                        if heads:
                            w(v.tensor_tensor_scan(M[0:m, 1:1 + P], neg[0:m, :], A[0:m, 1, :], -BIG, ALU.add, ALU.max))
                            w(v.tensor_tensor(T[0:m, :], M[0:m, 0:P], neg[0:m, :], ALU.add))
                            w(v.tensor_tensor(T[0:m, :], T[0:m, :], M[0:m, 1:1 + P], ALU.subtract))
                            v.tensor_tensor(U[0:m, :], A[0:m, 1, :], M[0:m, 1:1 + P], ALU.subtract).then_inc(s_va, 1)
                            v.wait_ge(s_act, 1)
                            w(v.tensor_tensor(U[0:m, :], U[0:m, :], A[0:m, 0, :], ALU.mult))
                            w(v.tensor_tensor_scan(S[0:m, 1:1 + P], T[0:m, :], U[0:m, :], 0.0, ALU.mult, ALU.add))
                            w(v.tensor_tensor(T[0:m, :], M[0:m, 0:P], nc_[0:m, :], ALU.add))
                            w(v.tensor_scalar(M[0:m, 1:1 + P], T[0:m, :], -BIG, None, ALU.max))
                        else:
                            w(v.tensor_tensor_scan(S[0:m, 1:1 + P], self.flag[0:m, :], A[0:m, 0, :], 0.0, ALU.mult, ALU.add))
                        w(v.tensor_tensor(T[0:m, :], S[0:m, 0:P], self.cont[0:m, :], ALU.mult))
                        v.tensor_copy(S[0:m, 1:1 + P], T[0:m, :]).then_inc(s_vp, 1)
                        v.wait_ge(s_pe, 2 * n + 2)
                        if n == 0:
                            v.wait_ge(s_g, 16)
                        if heads:
                            w(v.tensor_copy(heads_of(mx[:]), bcast(got[:, W:R].unsqueeze(2), [P, heads, F])))
                            w(v.tensor_tensor(mxr[:], mx[:], B[:, 1, 0:W], ALU.max))
                            w(v.tensor_tensor(T[:, 0:W], mx[:], mxr[:], ALU.subtract))
                            v.tensor_tensor(U[:, 0:W], B[:, 1, 0:W], mxr[:], ALU.subtract).then_inc(s_va, 1)
                            v.wait_ge(s_act, 2)
                            w(v.tensor_tensor(got[:, 0:W], got[:, 0:W], T[:, 0:W], ALU.mult))
                            w(v.tensor_tensor(U[:, 0:W], U[:, 0:W], B[:, 0, 0:W], ALU.mult))
                            v.tensor_tensor(got[:, 0:W], got[:, 0:W], U[:, 0:W], ALU.add)
                            v.tensor_copy(got[:, W:R].unsqueeze(2), heads_of(mxr[:])[:, :, 0:1]).then_inc(s_vp, 1)
                        else:
                            v.tensor_tensor(got[:, a:a + m], got[:, a:a + m], B[:, 0, 0:m], ALU.add).then_inc(s_vp, 1)

    def node_rows(self, rows, R, Y):
        nc = self.nc
        with ExitStack() as c:
            s_g = self.dsem("node_rows")
            with self.block() as block:
                @block.gpsimd
                def _(g):
                    for i in range(NT):
                        g.indirect_dma_start(Y[:, i, :], None, rows, bass.IndirectOffsetOnAxis(
                            ap=self.end_i[:, i:i + 1], axis=0)).then_inc(s_g, 16)
                    g.wait_ge(s_g, 16 * NT)

    def gat_edges(self, tab, WT, heads, F, starts, rows, ad_col, histogram):
        nc = self.nc
        W = heads * (F + 1)
        R = W + heads
        with ExitStack() as c:
            sb, sem = (lambda n, s, d=F32: self.sb(n, s, d, c)), (lambda n: self.sem(n, c))
            neg = sb("neg", [P, EP])
            IX = [sb(f"src_index{b}", [P, CH], I32) for b in range(2)]
            G = [sb(f"gathered{b}", [P, CH, WT]) for b in range(2)]
            ST = [sb(f"start_values{b}", [P, CH, heads]) for b in range(2)]
            AD = [sb(f"alpha_dst{b}", [P, heads, CH]) for b in range(2)]
            M = [sb(f"maxima{b}", [P, heads, 1 + CH]) for b in range(2)]
            X = sb("exponents", [P, 2, heads, CH])
            PR = sb("products", [P, F, CH])
            OUT = [sb(f"scanned{b}", [P, CH, R]) for b in range(2)]
            D0 = sb("first_dst_rows", [P, WT])
            s_ix = [sem(f"index_in{b}") for b in range(2)]
            s_st = [sem(f"starts_in{b}") for b in range(2)]
            s_g = [self.dsem(f"gathered{b}") for b in range(2)]
            s_o = [sem(f"rows_out{b}") for b in range(2)]
            s_used, s_v, s_e, s_x, s_done, s_pass = (sem(x) for x in (
                "inputs_used", "dve_chain", "exponents_ready", "exp_done", "rows_ready", "pool_passed"))
            s_d0 = self.dsem("first_dst_in")
            srcv = self.t["src"].rearrange("(p c) -> p c", p=P)
            stv = starts[0:E, :].rearrange("(p c) w -> p c w", p=P)
            outv = rows[0:E, :].rearrange("(p c) w -> p c w", p=P)
            if histogram:
                LO = sb("src_low_bits", [P, CH], I32)
                LOf = sb("src_low", [P, CH], BF16)
                HIf = sb("src_high", [P, CH], BF16)
                io = sb("iota_bf", [P, P], BF16)
                ioi = sb("iota_int", [P, P], I32)
                HG = 5
                OL = [sb(f"low_onehot{b}", [P, HG, P], BF16) for b in range(2)]
                OH = [sb(f"high_onehot{b}", [P, HG, NT], BF16) for b in range(2)]
                hp = self.ps("histogram", [P, 512], c)
                s_io, s_oh, s_ohu = (sem(x) for x in ("iota", "onehots_ready", "onehots_used"))
                assert NT * P >= N and NT <= P

            with self.block() as block:
                @block.sync
                def _(sp):
                    def load(k, b):
                        at, used = held(sp, k * CH, k - 1)
                        if not first(k, 2):
                            sp.wait_ge(s_used, used)
                        sp.dma_start(IX[b][:], srcv[:, ds(at, CH)]).then_inc(s_ix[b], 16)
                        sp.dma_start(ST[b][:], stv[:, ds(at, CH), :]).then_inc(s_st[b], 16)
                    chunks(sp, NCH, 3, load)

                @block.gpsimd
                def _(g):
                    if histogram:
                        g.iota(ioi[:], pattern=[[1, P]], base=0, channel_multiplier=0).then_inc(s_io, 1)
                    g.indirect_dma_start(D0[:], None, tab, bass.IndirectOffsetOnAxis(ap=self.dst0_i[:], axis=0)).then_inc(s_d0, 16)
                    def gather(k, b):
                        g.wait_ge(s_ix[b], (k - b) * 8 + 16)
                        g.sem_inc(s_pass, 1)
                        for j in range(CH):
                            g.indirect_dma_start(G[b][:, j, :], None, tab, bass.IndirectOffsetOnAxis(
                                ap=IX[b][:, j:j + 1], axis=0)).then_inc(s_g[b], 16)
                    chunks(g, NCH, 3, gather)

                @block.vector
                def _(v):
                    w0 = Chain(v, s_v)
                    v.tensor_scalar(neg[:], self.same[:], 1.0, BIG, ALU.subtract, ALU.mult)
                    v.memset(AD[1][:], 0.0)
                    v.memset(M[1][:], -BIG)
                    w0(v.memset(OUT[1][:], 0.0))
                    if histogram:
                        v.wait_ge(s_io, 1)
                        w0(v.tensor_copy(io[:], ioi[:]))
                    K = [0]

                    def count_src(k, b, w, idx):
                        w(v.tensor_scalar(LO[:], idx, P - 1, None, ALU.bitwise_and))
                        w(v.tensor_copy(LOf[:], LO[:]))
                        w(v.tensor_scalar(LO[:], idx, 7, None, ALU.logical_shift_right))
                        w(v.tensor_copy(HIf[:], LO[:]))
                        for q in range(CH // HG):
                            n = k * (CH // HG) + q
                            ob = (b * (CH // HG) + q) % 2
                            if not first(k, 1) or q >= 2:
                                v.wait_ge(s_ohu, n - 1)
                            a = q * HG
                            v.tensor_tensor(OL[ob][:], bcast(io[:].unsqueeze(1), [P, HG, P]),
                                            bcast(LOf[:, a:a + HG].unsqueeze(2), [P, HG, P]), ALU.is_equal)
                            v.tensor_tensor(OH[ob][:], bcast(io[:, 0:NT].unsqueeze(1), [P, HG, NT]),
                                            bcast(HIf[:, a:a + HG].unsqueeze(2), [P, HG, NT]), ALU.is_equal).then_inc(s_oh, 1)

                    def compute(k, b):
                        w = Chain(v, s_v, w0.n + k * K[0] if not first(k, 1) else w0.n)
                        sm, ng = self.same[:, ds(k * CH, CH)], neg[:, ds(k * CH, CH)]
                        m = k * 8 + 16 - 8 * b if not isinstance(k, int) else 16 * (k // 2 + 1)
                        v.wait_ge(s_st[b], m)
                        if first(k, 1):
                            v.wait_ge(s_d0, 16)
                            w(v.tensor_copy(ST[0][:, 0, :], D0[:, ad_col:ad_col + heads]))
                        else:
                            w(v.tensor_copy(M[b][:, :, 0:1], M[1 - b][:, :, CH:CH + 1]))
                        for h in range(heads):
                            ins = v.tensor_tensor_scan(AD[b][:, h, :], sm, ST[b][:, :, h], AD[1 - b][:, h, CH - 1:CH], ALU.mult, ALU.add)
                        w(ins)
                        v.wait_ge(s_g[b], m * CH)
                        w(v.tensor_tensor(AD_E(b), AD[b][:], G[b][:, :, 0:heads].rearrange("p c h -> p h c"), ALU.add))
                        w(v.scalar_tensor_tensor(EE[:], EE[:], 0.2, EE[:], ALU.mult, ALU.max))
                        if first(k, 1):
                            v.tensor_copy(M[b][:, :, 0:1], M[1 - b][:, :, CH:CH + 1])
                        for h in range(heads):
                            ins = v.tensor_tensor_scan(M[b][:, h, 1:1 + CH], ng, EE[:, h, :], M[1 - b][:, h, CH:CH + 1], ALU.add, ALU.max)
                        w(ins)
                        w(v.tensor_tensor(X[:, 0], M[b][:, :, 0:CH], bcast(ng.unsqueeze(1), [P, heads, CH]), ALU.add))
                        v.tensor_tensor(X[:, 0], X[:, 0], M[b][:, :, 1:1 + CH], ALU.subtract)
                        v.tensor_tensor(X[:, 1], EE[:], M[b][:, :, 1:1 + CH], ALU.subtract).then_inc(s_e, 1)
                        if histogram:
                            count_src(k, b, w, IX[b][:])
                        v.wait_ge(s_x, k + 1)
                        if not first(k, 2):
                            v.wait_ge(s_o[b], m - 16)
                        for h in range(heads):
                            w(v.tensor_tensor(PR[:], G[b][:, :, heads:heads + F].rearrange("p c f -> p f c"),
                                              bcast(X[:, 1, h, :].unsqueeze(1), [P, F, CH]), ALU.mult))
                            for f in range(F + 1):
                                col = h * (F + 1) + f
                                ins = v.tensor_tensor_scan(OUT[b][:, :, col], X[:, 0, h, :], X[:, 1, h, :] if f == 0 else PR[:, f - 1, :],
                                                           OUT[1 - b][:, CH - 1, col:col + 1], ALU.mult, ALU.add)
                            w(ins)
                        v.tensor_copy(OUT[b][:, :, W:R], M[b][:, :, 1:1 + CH].rearrange("p h c -> p c h")).then_inc(s_done, 1)
                        v.sem_inc(s_used, 1)
                        if first(k, 1):
                            K[0] = w.n
                        assert w.n == K[0]
                    EE = sb("scores", [P, heads, CH])
                    AD_E = lambda b: EE[:]
                    chunks(v, NCH, 3, compute)
                    v.wait_ge(s_done, NCH)
                    v.tensor_copy(self.tail[:, 0:R], OUT[(NCH - 1) % 2][:, CH - 1, :])

                @block.scalar
                def _(a):
                    def exps(k, b):
                        at = k * CH if isinstance(k, int) else a.snap(k * CH)
                        a.wait_ge(s_e, k + 1)
                        nc.scalar.activation(X[:], X[:], ACT.Exp).then_inc(s_x, 1)
                        a.wait_ge(s_done, k + 1)
                        a.dma_start(outv[:, ds(at, CH), :], OUT[b][:]).then_inc(s_o[b], 16)
                    chunks(a, NCH, 3, exps)
                    for b in range(2):
                        a.wait_ge(s_o[b], 16 * ((NCH + 1 - b) // 2))

                if histogram:
                    @block.tensor
                    def _(pe):
                        def count(k, b):
                            for q in range(CH // HG):
                                n = k * (CH // HG) + q
                                ob = (b * (CH // HG) + q) % 2
                                pe.wait_ge(s_oh, n + 1)
                                for j in range(HG):
                                    last = pe.matmul(hp[:, 0:NT], OL[ob][:, j, :], OH[ob][:, j, :],
                                                     start=first(k, 1) and q == 0 and j == 0,
                                                     stop=False, skip_group_check=True)
                                last.then_inc(s_ohu, 1)
                        chunks(pe, NCH, 3, count)

            if histogram:
                cnt = sb("counts", [P, NT])
                cT = sb("counts_T", [P, P])
                hd = self.dram("src_degree", (NP,))
                s1, s2, s3, s4 = (sem(x) for x in ("counts_ready", "counts_turned", "counts_out", "counts_in"))
                with self.block() as block:
                    @block.vector
                    def _(v):
                        v.tensor_copy(cnt[:], hp[:, 0:NT]).then_inc(s1, 1)
                        v.wait_ge(s2, 1)
                        v.tensor_copy(cT[0:NT, :], hp[0:NT, P:2 * P]).then_inc(s1, 1)

                    @block.tensor
                    def _(pe):
                        pe.wait_ge(s1, 1)
                        pe.transpose(hp[0:NT, P:2 * P], cnt[:], self.ident[:]).then_inc(s2, 1)

                    @block.sync
                    def _(sp):
                        sp.wait_ge(s1, 2)
                        sp.dma_start(hd.rearrange("(a b) -> a b", b=P), cT[0:NT, :]).then_inc(s3, 16)
                        sp.wait_ge(s3, 16)
                        sp.dma_start(self.deg_s[:], hd.rearrange("(p t) -> p t", p=P)).then_inc(s4, 16)
                        sp.wait_ge(s4, 16)
        self.fixup(rows, W, self.tail, heads)

    def gat_nodes(self, TN, heads, F, ad_col, rows, S):
        nc = self.nc
        W = heads * (F + 1)
        with ExitStack() as c:
            sb = lambda n, s: self.sb(n, s, F32, c)
            NE = sb("run_ends", [P, NT, W + heads])
            es = sb("self_score", [P, NT, heads])
            m = sb("max", [P, NT, heads])
            x = sb("exps", [P, 2, NT, heads])
            self.node_rows(rows, W + heads, NE)
            s_v, s_a, s_x = (self.sem(n, c) for n in ("dve_chain", "exponents_ready", "exp_done"))
            with self.block() as block:
                @block.vector
                def _(v):
                    w = Chain(v, s_v)
                    w(v.tensor_tensor(es[:], TN[:, :, 0:heads], TN[:, :, ad_col:ad_col + heads], ALU.add))
                    w(v.scalar_tensor_tensor(es[:], es[:], 0.2, es[:], ALU.mult, ALU.max))
                    w(v.tensor_tensor(m[:], es[:], NE[:, :, W:W + heads], ALU.max))
                    v.tensor_tensor(x[:, 0], NE[:, :, W:W + heads], m[:], ALU.subtract)
                    v.tensor_tensor(x[:, 1], es[:], m[:], ALU.subtract).then_inc(s_a, 1)
                    v.wait_ge(s_x, 1)
                    for h in range(heads):
                        z, s = NE[:, :, h * (F + 1)], NE[:, :, h * (F + 1) + 1:(h + 1) * (F + 1)]
                        o = S[:, :, h * F:(h + 1) * F]
                        v.tensor_tensor(m[:, :, h], z, x[:, 0, :, h], ALU.mult)
                        v.tensor_tensor(s, s, bcast(x[:, 0, :, h].unsqueeze(2), [P, NT, F]), ALU.mult)
                        w(v.tensor_tensor(o, TN[:, :, heads:heads + F], bcast(x[:, 1, :, h].unsqueeze(2), [P, NT, F]), ALU.mult))
                        v.tensor_tensor(o, o, s, ALU.add)
                        w(v.tensor_tensor(m[:, :, h], m[:, :, h], x[:, 1, :, h], ALU.add))
                        w(v.tensor_scalar(m[:, :, h], m[:, :, h], 1e-16, None, ALU.add))
                        w(v.reciprocal(m[:, :, h], m[:, :, h]))
                        w(v.tensor_tensor(o, o, bcast(m[:, :, h].unsqueeze(2), [P, NT, F]), ALU.mult))

                @block.scalar
                def _(a):
                    a.wait_ge(s_a, 1)
                    nc.scalar.activation(x[:], x[:], ACT.Exp).then_inc(s_x, 1)

    def selu(self, Y, W):
        nc = self.nc
        lam, alpha = 1.0507009873554805, 1.6732632423543772
        with ExitStack() as c:
            T = self.sb("negative_part", [P, NT, W], F32, c)
            s_v, s_a, s_x = (self.sem(n, c) for n in ("dve_chain", "negative_ready", "exp_done"))
            with self.block() as block:
                @block.vector
                def _(v):
                    w = Chain(v, s_v)
                    v.tensor_scalar(T[:], Y, 0.0, None, ALU.min).then_inc(s_a, 1)
                    w(v.tensor_scalar(Y, Y, 0.0, lam, ALU.max, ALU.mult))
                    v.wait_ge(s_x, 1)
                    w(v.tensor_scalar(T[:], T[:], 1.0, lam * alpha, ALU.subtract, ALU.mult))
                    w(v.tensor_tensor(Y, Y, T[:], ALU.add))

                @block.scalar
                def _(a):
                    a.wait_ge(s_a, 1)
                    nc.scalar.activation(T[:], T[:], ACT.Exp).then_inc(s_x, 1)

    def layer0(self):
        nc, t = self.nc, self.t
        F2 = 32
        with ExitStack() as c:
            sb = lambda n, s: self.sb(n, s, F32, c)
            W1 = sb("W1", [D, 96])
            W1b = sb("W1_blocks", [3 * D, 96])
            ab = sb("a_rows", [96, 4 * 96])
            wp = sb("w_times_a", [96, 96])
            W1x = sb("W1_alpha", [D, 2 * 3 + D])
            W2x = sb("W2_alpha", [96, F2 + 2])
            Wf = sb("Wf", [F2, D])
            b1, b2, bf = sb("b1", [P, 96]), sb("b2", [P, F2]), sb("bf", [P, D])
            s_w, s_v, s_z = (self.sem(n, c) for n in ("weights_in", "dve_chain", "cleared"))
            row = lambda ap, n, p: bcast(ap.rearrange("(a n) -> a n", a=1), [p, n])
            with self.block() as block:
                @block.sync
                def _(sp):
                    sp.wait_ge(s_z, 1)
                    loads = [(W1[:], t["L0_gnn_W1"]), (W2x[:, 1:1 + F2], t["L0_gnn_W2"]), (Wf[:], t["L0_gnn_Wf"])]
                    loads += [(W1b[h * D:(h + 1) * D, h * 32:(h + 1) * 32], t["L0_gnn_W1"][:, h * 32:(h + 1) * 32]) for h in range(3)]
                    loads += [(b1[:], row(t["L0_gnn_b1"], 96, P)), (b2[:], row(t["L0_gnn_b2"], F2, P)), (bf[:], row(t["L0_gnn_bf"], D, P))]
                    for i, (n, m) in enumerate((("a_src1", D), ("a_dst1", D), ("a_src2", 96), ("a_dst2", 96))):
                        a = t["L0_gnn_" + n].rearrange("h c -> (h c)")
                        k = a.shape[0]
                        loads.append((ab[0:m, i * 96:i * 96 + k], row(a, k, m)))
                    for dst, src in loads:
                        sp.dma_start(dst, src).then_inc(s_w, 16)
                    sp.wait_ge(s_w, 16 * len(loads))

                @block.vector
                def _(v):
                    v.memset(W1b[:], 0.0).then_inc(s_z, 1)
            with self.block() as block:
                @block.vector
                def _(v):
                    w = Chain(v, s_v)
                    for i in range(2):
                        w(v.tensor_tensor(wp[0:D, :], W1[:], ab[0:D, i * 96:(i + 1) * 96], ALU.mult))
                        w(v.tensor_reduce(W1x[:, 3 * i:3 * i + 3], wp[0:D, :].rearrange("p (h c) -> p h c", h=3), AX.X, ALU.add))
                    for i in range(2):
                        w(v.tensor_tensor(wp[:, 0:F2], W2x[:, 1:1 + F2], ab[:, (2 + i) * 96:(2 + i) * 96 + F2], ALU.mult))
                        w(v.tensor_reduce(W2x[:, i * (F2 + 1):i * (F2 + 1) + 1], wp[:, 0:F2], AX.X, ALU.add))
            rows1 = self.dram("gat1_rows", (E + 1, 3 * (D + 1) + 3))
            tab1 = self.dram("gat1_table", (NP, 6 + D))
            S1 = sb("S1", [P, NT, 3 * D])
            with ExitStack() as c2:
                T1 = self.sb("T1", [P, NT, 6 + D], F32, c2)
                Y = self.sb("alphas", [P, NT, 6], F32, c2)
                self.linear(self.H, D, W1x[:, 0:6], 6, Y)
                s_c = self.sem("table_ready", c2)
                with self.block() as block:
                    @block.vector
                    def _(v):
                        v.tensor_copy(T1[:, :, 0:3], Y[:, :, 0:3])
                        v.tensor_copy(T1[:, :, 3:3 + D], self.H[:])
                        v.tensor_copy(T1[:, :, 3 + D:6 + D], Y[:, :, 3:6]).then_inc(s_c, 1)
                self.table(T1, 6 + D, tab1, self.starts3, 3 + D, 3)
                self.gat_edges(tab1, 6 + D, 3, D, self.starts3, rows1, 3 + D, True)
                self.gat_nodes(T1, 3, D, 3 + D, rows1, S1)
            rows2 = self.dram("gat2_rows", (E + 1, F2 + 2))
            tab2 = self.dram("gat2_table", (NP, F2 + 2))
            S2 = sb("S2", [P, NT, F2])
            with ExitStack() as c2:
                T2 = self.sb("T2", [P, NT, F2 + 2], F32, c2)
                with ExitStack() as c3:
                    Y1 = self.sb("Y1", [P, NT, 96], F32, c3)
                    self.linear(S1, 3 * D, W1b[:], 96, Y1, bias=b1[:])
                    self.selu(Y1[:], 96)
                    self.linear(Y1, 96, W2x[:], F2 + 2, T2)
                self.table(T2, F2 + 2, tab2, self.starts1, F2 + 1, 1)
                self.gat_edges(tab2, F2 + 2, 1, F2, self.starts1, rows2, F2 + 1, False)
                self.gat_nodes(T2, 1, F2, F2 + 1, rows2, S2)
            s_b = self.sem("biased", c)
            with self.block() as block:
                @block.vector
                def _(v):
                    v.tensor_tensor(S2[:], S2[:], bcast(b2[:].unsqueeze(1), [P, NT, F2]), ALU.add).then_inc(s_b, 1)
            self.selu(S2[:], F2)
            self.linear(S2, F2, Wf[:], D, self.H, bias=bf[:])
            s_r = self.sem("residual", c)
            with self.block() as block:
                @block.vector
                def _(v):
                    v.tensor_tensor(self.X[:], self.X[:], self.H[:], ALU.add).then_inc(s_r, 1)

    def scatter_buffers(self, c, find_first):
        sb, sem = (lambda n, s, d=F32: self.sb(n, s, d, c)), (lambda n: self.sem(n, c))
        o = type("Scatter", (), {})()
        o.find_first = find_first
        o.groups = -(-CH // 4)
        o.VAL = sb("edge_values", [P, CH, D])
        o.SV = [sb(f"column_sums{b}", [P, CH, D]) for b in range(2)]
        o.IXS = [sb(f"sum_rows{b}", [P, CH], I32) for b in range(2)]
        o.nq = 2 if find_first else 4
        o.EQ = [sb(f"equal_src{b}", [P, 4, P]) for b in range(o.nq)]
        if find_first:
            o.EL = sb("equal_earlier", [P, 4, P])
            o.CNT = sb("earlier", [P, CH])
            o.DT = sb("row_change", [P, CH])
        o.row_ps = [self.ps(f"src_row{b}", [P, 512], c) for b in range(2)]
        o.sum_ps = self.ps("column_sum", [P, 2, 256], c)
        o.s_val, o.s_row, o.s_eq, o.s_sum, o.s_sv, o.s_ixs, o.s_chunk, o.s_pass = (sem(x) for x in (
            "edge_values_ready", "src_rows_ready", "equality_ready", "sums_ready", "sums_copied", "sum_rows_ready",
            "chunk_added", "pool_passed"))
        o.s_add = [self.dsem(f"added{s}") for s in range(SETS)]
        return o

    def scatter_pe(self, pe, o, k):
        def rows(q):
            n = min(4, CH - 4 * q)
            for j in range(n):
                last = pe.matmul(o.row_ps[q % 2][:, j * P:(j + 1) * P], bcast(o.SRC[:, 4 * q + j:4 * q + j + 1], [P, P]),
                                 self.ident[:], start=True, stop=True)
            last.then_inc(o.s_row, 1)
        if not first(k, 1):
            pe.wait_ge(o.s_eq, k * o.groups)
        pe.wait_ge(o.s_src, k + 1)
        rows(0)
        rows(1)
        for q in range(o.groups):
            n = min(4, CH - 4 * q)
            pe.wait_ge(o.s_eq, k * o.groups + (q + 1))
            if q == 0:
                pe.wait_ge(o.s_val, k + 1)
            if not first(k, 1) or q >= 1:
                pe.wait_ge(o.s_sv, k * o.groups + q)
            for j in range(n):
                last = pe.matmul(o.sum_ps[:, q % 2, j * D:(j + 1) * D], o.EQ[q % 2][:, j, :], o.VAL[:, 4 * q + j, :],
                                 start=True, stop=True)
            last.then_inc(o.s_sum, 1)
            if q + 2 < o.groups:
                rows(q + 2)

    def scatter_dve(self, v, w, o, k, b):
        for q in range(o.groups):
            n = min(4, CH - 4 * q)
            v.wait_ge(o.s_row, k * o.groups + (q + 1))
            if not first(k, 1) or q >= 2:
                v.wait_ge(o.s_sum, k * o.groups + (q - 1))
            v.tensor_tensor(o.EQ[q % 2][:, 0:n, :], o.row_ps[q % 2][:, 0:n * P].rearrange("p (a b) -> p a b", b=P),
                            bcast(o.SRC[:, 4 * q:4 * q + n].unsqueeze(2), [P, n, P]), ALU.is_equal).then_inc(o.s_eq, 1)
            if o.find_first:
                v.wait_ge(o.s_eq, k * o.groups + (q + 1))
                w(v.tensor_tensor(o.EL[:, 0:n, :], o.EQ[q % 2][:, 0:n, :], bcast(self.lower[:].unsqueeze(1), [P, n, P]), ALU.mult))
                w(v.tensor_reduce(o.CNT[:, 4 * q:4 * q + n], o.EL[:, 0:n, :], AX.X, ALU.add))
        if not first(k, 2):
            v.wait_ge(o.s_chunk, k - 1)
        if o.find_first:
            w(v.tensor_scalar(o.CNT[:], o.CNT[:], 0.5, None, ALU.is_gt))
            w(v.tensor_scalar(o.DT[:], o.SRC[:], -1.0, self.trash[:], ALU.mult, ALU.add))
            w(v.tensor_tensor(o.DT[:], o.DT[:], o.CNT[:], ALU.mult))
            w(v.tensor_tensor(o.IXS[b][:], o.DT[:], o.SRC[:], ALU.add))
            w(v.tensor_copy(self.sidx[:, ds(k * CH, CH)], o.IXS[b][:]))
            v.sem_inc(o.s_ixs, 1)
        else:
            v.tensor_copy(o.IXS[b][:], self.sidx[:, ds(k * CH, CH)]).then_inc(o.s_ixs, 1)

    def scatter_act(self, a, o, k, b):
        if not first(k, 2):
            a.wait_ge(o.s_chunk, k - 1)
        for q in range(o.groups):
            n = min(4, CH - 4 * q)
            a.wait_ge(o.s_sum, k * o.groups + (q + 1))
            self.nc.scalar.activation(o.SV[b][:, 4 * q:4 * q + n, :], o.sum_ps[:, q % 2, 0:n * D].rearrange("p (a b) -> p a b", b=D),
                                      ACT.Copy).then_inc(o.s_sv, 1)

    def scatter_pool(self, g, o, k, b):
        g.wait_ge(o.s_ixs, k + 1)
        rounds = CH // PER_SET
        assert rounds % 2 == 1 and SETS == 2
        for q in range(rounds):
            s = (b + q) % SETS
            g.wait_ge(o.s_sv, k * o.groups + -(-(q + 1) * PER_SET // 4))
            g.sem_inc(o.s_pass, 1)
            if not first(k, 1) or q >= SETS:
                g.wait_ge(o.s_add[s], k * (rounds * 8 * PER_SET) + (q - s) * 8 * PER_SET)
                g.sem_inc(o.s_pass, 1)
            if q == 1 and not first(k, 1):
                g.sem_inc(o.s_chunk, 1)
            for i in range(PER_SET):
                j = q * PER_SET + i
                g.indirect_dma_start(self.acc[s * PER_SET + i], bass.IndirectOffsetOnAxis(ap=o.IXS[b][:, j:j + 1], axis=0),
                                     o.SV[b][:, j, :], None, compute_op=ALU.add).then_inc(o.s_add[s], 16)
        if isinstance(k, int) and k == NCH - 1:
            for s in range(SETS):
                g.wait_ge(o.s_add[s], (NCH * rounds + 1 - s) // 2 * 16 * PER_SET)

    def sum_accumulators(self, A, clear):
        nc = self.nc
        with ExitStack() as c:
            B = [self.sb(f"acc_in{i}", [P, NT, D], F32, c) for i in range(2)]
            zer = self.sb("zeros", [P, (NP + P) * D // P], F32, c)
            s_in = [self.sem(f"acc_in{i}", c) for i in range(2)]
            s_v, s_z, s_c = (self.sem(n, c) for n in ("summed", "zeros_ready", "cleared"))
            with self.block() as block:
                @block.sync
                def _(sp):
                    for i, a in enumerate(self.acc):
                        if i >= 2:
                            sp.wait_ge(s_v, i - 1)
                        sp.dma_start(B[i % 2][:], a[0:NP, :].rearrange("(p t) w -> p t w", p=P)).then_inc(s_in[i % 2], 16)
                    if clear:
                        sp.wait_ge(s_z, 1)
                        sp.wait_ge(s_v, len(self.acc))
                        for a in self.acc:
                            sp.dma_start(a.rearrange("(p c) w -> p (c w)", p=P), zer[:]).then_inc(s_c, 16)
                        sp.wait_ge(s_c, 16 * len(self.acc))

                @block.vector
                def _(v):
                    v.memset(zer[:], 0.0).then_inc(s_z, 1)
                    for i in range(len(self.acc)):
                        v.wait_ge(s_in[i % 2], 16 * (i // 2 + 1))
                        if i:
                            v.wait_ge(s_v, i)
                            v.tensor_tensor(A[:], A[:], B[i % 2][:], ALU.add).then_inc(s_v, 1)
                        else:
                            v.tensor_copy(A[:], B[0][:]).then_inc(s_v, 1)

    def layer1(self):
        nc, t = self.nc, self.t
        HD = 64
        W = D + 1
        with ExitStack() as c:
            sbp = lambda n, s, d=F32: self.sb(n, s, d, c)
            DI = sbp("dst_norm", [P, NT])
            self.tab17 = self.dram("sheaf_table", (NP, W))
            rows = self.dram("sheaf_rows", (E + 1, D))
            W1z = sbp("W1_at", [P, 4, P])
            W2b = sbp("W2_blocks", [P, 2 * D])
            b1 = sbp("b1", [P, 1])
            b2 = sbp("b2", [P, 2 * D])
            with ExitStack() as c2:
                T17 = self.sb("T17", [P, NT, W], F32, c2)
                dg = self.sb("degree", [P, NT], F32, c2)
                r = self.sb("root", [P, NT], F32, c2)
                r2 = self.sb("newton", [P, NT], F32, c2)
                s_w, s_v, s_z, s_a, s_x = (self.sem(n, c2) for n in ("weights_in", "dve_chain", "cleared", "degree_ready", "root_ready"))
                with self.block() as block:
                    @block.vector
                    def _(v):
                        w = Chain(v, s_v)
                        v.memset(W1z[:], 0.0)
                        v.memset(W2b[:], 0.0).then_inc(s_z, 1)
                        w(v.tensor_tensor(dg[:], self.deg_d[:], self.deg_s[:], ALU.add))
                        v.tensor_scalar(dg[:], dg[:], 1e-5, None, ALU.max).then_inc(s_a, 1)
                        v.wait_ge(s_x, 1)
                        w(v.reciprocal(r[:], r[:]))
                        w(v.tensor_tensor(r2[:], r[:], r[:], ALU.mult))
                        w(v.tensor_tensor(r2[:], r2[:], dg[:], ALU.mult))
                        w(v.tensor_scalar(r2[:], r2[:], -0.5, 1.5, ALU.mult, ALU.add))
                        w(v.tensor_tensor(DI[:], r[:], r2[:], ALU.mult))
                        v.tensor_copy(T17[:, :, 0], DI[:])
                        w(v.tensor_copy(T17[:, :, 1:W], self.H[:]))

                    @block.scalar
                    def _(a):
                        a.wait_ge(s_a, 1)
                        nc.scalar.activation(r[:], dg[:], ACT.Sqrt).then_inc(s_x, 1)

                    @block.sync
                    def _(sp):
                        sp.wait_ge(s_z, 1)
                        n = 0
                        w1 = t["L1_gnn_W1"].rearrange("m k -> k m")
                        w2 = t["L1_gnn_W2"].rearrange("d k -> k d")
                        col = lambda ap: ap.rearrange("(n a) -> n a", a=1)
                        row = lambda ap, n: bcast(ap.rearrange("(a n) -> a n", a=1), [P, n])
                        loads = []
                        for j in range(4):
                            for side in range(2):
                                for r_ in range(2):
                                    other = (side + r_) % 2
                                    loads.append((W1z[32 * j + D * side:32 * j + D * side + D, j, HD * r_:HD * r_ + HD],
                                                  w1[D * other:D * other + D, :]))
                        for r_ in range(2):
                            loads.append((W2b[HD * r_:HD * r_ + HD, D * r_:D * r_ + D], w2))
                            loads.append((b1[HD * r_:HD * r_ + HD, :], col(t["L1_gnn_b1"])))
                            loads.append((b2[:, D * r_:D * r_ + D], row(t["L1_gnn_b2"], D)))
                        with nc.allow_non_contiguous_dma(reason="small weights, transposed as they are loaded"):
                            for dst, src in loads:
                                sp.dma_start(dst, src).then_inc(s_w, 16)
                        sp.wait_ge(s_w, 16 * len(loads))
                self.table(T17, W, self.tab17, self.starts17, 0, W)
            self.sheaf_edges(rows, W1z, W2b, b1, b2)
            with ExitStack() as c2:
                NE = self.sb("run_ends", [P, NT, D], F32, c2)
                A = self.sb("src_sums", [P, NT, D], F32, c2)
                self.node_rows(rows, D, NE)
                self.sum_accumulators(A, True)
                s_v = self.sem("dve_chain", c2)
                with self.block() as block:
                    @block.vector
                    def _(v):
                        w = Chain(v, s_v)
                        w(v.tensor_tensor(A[:], A[:], NE[:], ALU.add))
                        w(v.tensor_tensor(A[:], A[:], bcast(DI[:].unsqueeze(2), [P, NT, D]), ALU.mult))
                        w(v.tensor_tensor(A[:], A[:], self.H[:], ALU.add))
                        w(v.tensor_scalar(A[:], A[:], 0.0, None, ALU.max))
                        w(v.tensor_tensor(self.X[:], self.X[:], A[:], ALU.add))

    def sheaf_edges(self, rows, W1z, W2b, b1, b2):
        nc = self.nc
        W = D + 1
        SG = 8
        CP = 16 * SG
        with ExitStack() as c:
            sb, sem = (lambda n, s, d=F32: self.sb(n, s, d, c)), (lambda n: self.sem(n, c))
            IX = [sb(f"src_index{b}", [P, CH], I32) for b in range(2)]
            G = [sb(f"gathered{b}", [P, CH, W]) for b in range(2)]
            ST = sb("start_values", [P, CH, W])
            DD = [sb(f"dst_norm{b}", [P, CH]) for b in range(2)]
            DL = [sb(f"last_dst{b}", [P, D]) for b in range(2)]
            SN = sb("src_norm", [P, CH])
            XY = sb("src_dst", [P, CP, 2 * D])
            V = sb("vectors", [P, CP, 2 * D])
            Q = sb("products", [P, CH, 2 * D])
            Y = sb("reflected", [P, CH, 2 * D])
            n2, tt = sb("norms", [P, CH, 2]), sb("dots", [P, CH, 2])
            OUT = [sb(f"scanned{b}", [P, CH, D]) for b in range(2)]
            XT = sb("xyT", [P, 512])
            R = [sb(f"hidden{b}", [P, 512]) for b in range(2)]
            D0 = sb("first_dst_rows", [P, W])
            o = self.scatter_buffers(c, True)
            srcc = sb("src_chunk", [P, CH])
            o.SRC = srcc
            tp = self.ps("xyT_ps", [P, 512], c)
            pre = [self.ps(f"hidden_ps{b}", [P, 512], c) for b in range(2)]
            vp = [self.ps(f"vectors_ps{b}", [P, 512], c) for b in range(2)]
            s_ix = [sem(f"index_in{b}") for b in range(2)]
            s_st = sem("starts_in")
            s_g = [self.dsem(f"gathered{b}") for b in range(2)]
            s_o = [sem(f"rows_out{b}") for b in range(2)]
            (s_used, s_v, s_xy, s_t, s_xt, s_pre, s_r, s_vm, s_vc, s_done, s_pass, s_stu) = (sem(x) for x in (
                "inputs_used", "dve_chain", "src_dst_ready", "transposed", "transposed_copied", "hidden_ready",
                "hidden_copied", "hidden_used", "vectors_copied", "rows_ready",
                "pool_passed", "starts_used"))
            s_d0 = self.dsem("first_dst_in")
            o.s_src = s_xy
            srcv = self.t["src"].rearrange("(p c) -> p c", p=P)
            stv = self.starts17[0:E, :].rearrange("(p c) w -> p c w", p=P)
            outv = rows[0:E, :].rearrange("(p c) w -> p c w", p=P)
            with self.block() as block:
                @block.sync
                def _(sp):
                    def load(k, b):
                        at, before, last = held(sp, k * CH, k - 1, k * 1)
                        if not first(k, 2):
                            sp.wait_ge(s_used, before)
                        sp.dma_start(IX[b][:], srcv[:, ds(at, CH)]).then_inc(s_ix[b], 16)
                        if not first(k, 1):
                            sp.wait_ge(s_stu, last)
                        sp.dma_start(ST[:], stv[:, ds(at, CH), :]).then_inc(s_st, 16)
                    chunks(sp, NCH, 3, load)

                @block.gpsimd
                def _(g):
                    g.indirect_dma_start(D0[:], None, self.tab17, bass.IndirectOffsetOnAxis(ap=self.dst0_i[:], axis=0)).then_inc(s_d0, 16)
                    def gather(k, b):
                        g.wait_ge(s_ix[b], (k - b) * 8 + 16)
                        g.sem_inc(s_pass, 1)
                        for j in range(CH):
                            g.indirect_dma_start(G[b][:, j, :], None, self.tab17, bass.IndirectOffsetOnAxis(
                                ap=IX[b][:, j:j + 1], axis=0)).then_inc(s_g[b], 16)
                        if not first(k, 2):
                            self.scatter_pool(g, o, k - 2, b)
                    chunks(g, NCH, 3, gather)
                    for k in (NCH - 2, NCH - 1):
                        self.scatter_pool(g, o, k, k % 2)

                @block.tensor
                def _(pe):
                    def products(k, b):
                        pe.wait_ge(s_xy, k + 1)
                        for q in range(SG):
                            if not first(k, 1) or q >= 1:
                                pe.wait_ge(s_xt, k * SG + q)
                            for i in range(4):
                                last = pe.transpose(tp[:, i * P:(i + 1) * P],
                                                    XY[:, 16 * q + 4 * i:16 * q + 4 * i + 4, :].rearrange("p a f -> p (a f)"), self.ident[:])
                            last.then_inc(s_t, 1)
                            pe.wait_ge(s_xt, k * SG + (q + 1))
                            if not first(k, 1) or q >= 2:
                                pe.wait_ge(s_vc, k * SG + (q - 1))
                            def second(j):
                                n = q * 4 + j
                                pe.wait_ge(s_r, k * (4 * SG) + (n + 1))
                                for i in range(4):
                                    last = pe.matmul(vp[q % 2][:, (4 * i + j) * 32:(4 * i + j + 1) * 32], R[j % 2][:, i * P:(i + 1) * P],
                                                     W2b[:], start=True, stop=True)
                                last.then_inc(s_vm, 1)
                            for j in range(4):
                                n = q * 4 + j
                                if not first(k, 1) or n >= 2:
                                    pe.wait_ge(s_r, k * (4 * SG) + (n - 1))
                                pe.matmul(pre[j % 2][:], W1z[:, j, :], XT[:], start=True, stop=True).then_inc(s_pre, 1)
                                if j:
                                    second(j - 1)
                            second(3)
                        self.scatter_pe(pe, o, k)
                    chunks(pe, NCH, 3, products)

                @block.scalar
                def _(a):
                    def step(k, b):
                        at = k * CH if isinstance(k, int) else a.snap(k * CH)
                        for q in range(SG):
                            a.wait_ge(s_t, k * SG + (q + 1))
                            if not first(k, 1) or q >= 1:
                                a.wait_ge(s_pre, k * (4 * SG) + 4 * q)
                            nc.scalar.activation(XT[:], tp[:], ACT.Copy).then_inc(s_xt, 1)
                            for j in range(4):
                                n = q * 4 + j
                                a.wait_ge(s_pre, k * (4 * SG) + (n + 1))
                                if not first(k, 1) or n >= 2:
                                    a.wait_ge(s_vm, k * (4 * SG) + (n - 1))
                                nc.scalar.activation(R[j % 2][:], pre[j % 2][:], ACT.Relu, bias=b1[:]).then_inc(s_r, 1)
                        self.scatter_act(a, o, k, b)
                        a.wait_ge(s_done, k + 1)
                        a.dma_start(outv[:, ds(at, CH), :], OUT[b][:]).then_inc(s_o[b], 16)
                    chunks(a, NCH, 3, step)
                    for b in range(2):
                        a.wait_ge(s_o[b], 16 * ((NCH + 1 - b) // 2))

                @block.vector
                def _(v):
                    w0 = Chain(v, s_v)
                    v.memset(XY[:], 0.0)
                    v.memset(DD[1][:], 0.0)
                    v.memset(DL[1][:], 0.0)
                    w0(v.memset(OUT[1][:], 0.0))
                    K = [0]

                    def compute(k, b):
                        w = Chain(v, s_v, w0.n + k * K[0] if not first(k, 1) else w0.n)
                        sm = self.same[:, ds(k * CH, CH)]
                        m = k * 8 + 16 - 8 * b if not isinstance(k, int) else 16 * (k // 2 + 1)
                        v.wait_ge(s_st, k * 16 + 16)
                        if first(k, 1):
                            v.wait_ge(s_d0, 16)
                            w(v.tensor_copy(ST[:, 0, :], D0[:]))
                        else:
                            v.wait_ge(s_vc, k * SG)
                            w(v.tensor_copy(tt[:, 0:1, 0], DD[1 - b][:, CH - 1:CH]))
                        v.tensor_tensor_scan(DD[b][:], sm, ST[:, :, 0], DD[1 - b][:, CH - 1:CH], ALU.mult, ALU.add)
                        for f in range(D):
                            ins = v.tensor_tensor_scan(XY[:, 0:CH, D + f], sm, ST[:, :, 1 + f], DL[1 - b][:, f:f + 1], ALU.mult, ALU.add)
                        w(ins)
                        v.tensor_copy(DL[b][:], XY[:, CH - 1, D:2 * D]).then_inc(s_stu, 1)
                        v.wait_ge(s_g[b], m * CH)
                        v.tensor_copy(srcc[:], self.srcf[:, ds(k * CH, CH)])
                        v.tensor_copy(XY[:, 0:CH, 0:D], G[b][:, :, 1:W]).then_inc(s_xy, 1)
                        w(v.tensor_copy(SN[:], G[b][:, :, 0]))
                        v.sem_inc(s_used, 1)
                        for q in range(SG):
                            v.wait_ge(s_vm, k * (4 * SG) + 4 * (q + 1))
                            v.tensor_tensor(V[:, 16 * q:16 * q + 16, :], vp[q % 2][:].rearrange("p (a f) -> p a f", f=2 * D),
                                            bcast(b2[:].unsqueeze(1), [P, 16, 2 * D]), ALU.add).then_inc(s_vc, 1)
                        v.wait_ge(s_vc, k * SG + SG)
                        pair = lambda ap: ap.rearrange("p c (a f) -> p c a f", a=2)
                        VV, XX = V[:, 0:CH, :], XY[:, 0:CH, :]
                        spread = lambda ap: bcast(ap.unsqueeze(3), [P, CH, 2, D])
                        w(v.tensor_tensor(Q[:], VV, VV, ALU.mult))
                        w(v.tensor_reduce(n2[:], pair(Q[:]), AX.X, ALU.add))
                        w(v.tensor_scalar(n2[:], n2[:], 1e-24, None, ALU.max))
                        w(v.reciprocal(n2[:], n2[:]))
                        w(v.tensor_tensor(Q[:], VV, XX, ALU.mult))
                        w(v.tensor_reduce(tt[:], pair(Q[:]), AX.X, ALU.add))
                        w(v.scalar_tensor_tensor(tt[:], tt[:], -2.0, n2[:], ALU.mult, ALU.mult))
                        w(v.tensor_tensor(pair(Q[:]), pair(VV), spread(tt[:]), ALU.mult))
                        w(v.tensor_tensor(Y[:], XX, Q[:], ALU.add))
                        w(v.tensor_tensor(Q[:, :, 0:D], V[:, 0:CH, 0:D], Y[:, :, D:2 * D], ALU.mult))
                        w(v.tensor_tensor(Q[:, :, D:2 * D], V[:, 0:CH, D:2 * D], Y[:, :, 0:D], ALU.mult))
                        w(v.tensor_reduce(tt[:], pair(Q[:]), AX.X, ALU.add))
                        w(v.scalar_tensor_tensor(tt[:], tt[:], -2.0, n2[:], ALU.mult, ALU.mult))
                        w(v.tensor_tensor(pair(Q[:]), pair(VV), spread(tt[:]), ALU.mult))
                        w(v.tensor_tensor(Q[:, :, 0:D], Q[:, :, 0:D], Y[:, :, D:2 * D], ALU.add))
                        w(v.tensor_tensor(Q[:, :, D:2 * D], Q[:, :, D:2 * D], Y[:, :, 0:D], ALU.add))
                        if not first(k, 1):
                            v.wait_ge(o.s_sum, k * o.groups)
                        w(v.tensor_tensor(o.VAL[:], Q[:, :, 0:D], bcast(DD[b][:].unsqueeze(2), [P, CH, D]), ALU.mult))
                        v.sem_inc(o.s_val, 1)
                        w(v.tensor_tensor(Q[:, :, D:2 * D], Q[:, :, D:2 * D], bcast(SN[:].unsqueeze(2), [P, CH, D]), ALU.mult))
                        if not first(k, 2):
                            v.wait_ge(s_o[b], m - 16)
                        for f in range(D):
                            ins = v.tensor_tensor_scan(OUT[b][:, :, f], sm, Q[:, :, D + f], OUT[1 - b][:, CH - 1, f:f + 1], ALU.mult, ALU.add)
                        w(ins)
                        v.sem_inc(s_done, 1)
                        self.scatter_dve(v, w, o, k, b)
                        if first(k, 1):
                            K[0] = w.n
                        assert w.n == K[0]
                    chunks(v, NCH, 3, compute)
                    v.tensor_copy(self.tail[:, 0:D], OUT[(NCH - 1) % 2][:, CH - 1, :])
        self.fixup(rows, D, self.tail)

    def layer2(self):
        nc, t = self.nc, self.t
        NE_ = 8
        W = D + 1
        with ExitStack() as c:
            sb = lambda n, s: self.sb(n, s, F32, c)
            Wm = sb("W_message", [D * NE_, D])
            Wl = sb("W_message_lin", [D, D])
            Wu = [sb(f"W_update{i}", [P, D]) for i in range(2)]
            Wo = sb("W_update_lin", [D, D])
            with ExitStack() as c2:
                T17 = self.sb("T17", [P, NT, W], F32, c2)
                s_w, s_v = (self.sem(n, c2) for n in ("weights_in", "dve_chain"))
                wu = t["L2_gnn_W_upd_tp"].rearrange("i h k -> (i h) k")
                loads = [(Wm[:], t["L2_gnn_W_msg_tp"].rearrange("i j h -> (i j) h")), (Wl[:], t["L2_gnn_W_msg_lin"]),
                         (Wu[0][:], wu[0:P, :]), (Wu[1][:], wu[P:2 * P, :]), (Wo[:], t["L2_gnn_W_upd_lin"])]
                with self.block() as block:
                    @block.sync
                    def _(sp):
                        for dst, src in loads:
                            sp.dma_start(dst, src).then_inc(s_w, 16)
                        sp.wait_ge(s_w, 16 * len(loads))

                    @block.vector
                    def _(v):
                        w = Chain(v, s_v)
                        v.memset(T17[:, :, 0:1], 0.0)
                        w(v.tensor_copy(T17[:, :, 1:W], self.H[:]))
                        v.wait_ge(s_w, 16 * len(loads))
                        w(v.tensor_scalar(Wl[:], Wl[:], D ** -0.5, None, ALU.mult))
                        w(v.tensor_scalar(Wo[:], Wo[:], D ** -0.5, None, ALU.mult))
                self.table(T17, W, self.tab17, self.starts17, 0, W)
            self.message_edges(Wm, NE_)
            with ExitStack() as c2:
                A = self.sb("src_sums", [P, NT, D], F32, c2)
                B = self.sb("messages", [P, NT, D], F32, c2)
                OP = self.sb("outer", [P, NT, P], F32, c2)
                U = self.sb("update", [P, NT, D], F32, c2)
                self.sum_accumulators(A, False)
                self.linear(A, D, Wl[:], D, B)
                for half in range(2):
                    s_v = self.sem("outer_ready", c2)
                    with self.block() as block:
                        @block.vector
                        def _(v):
                            for i in range(8):
                                ins = v.tensor_tensor(OP[:, :, i * D:(i + 1) * D], B[:],
                                                      bcast(self.H[:, :, 8 * half + i:8 * half + i + 1], [P, NT, D]), ALU.mult)
                            ins.then_inc(s_v, 1)
                    self.linear(OP, P, Wu[half][:], D, U, add=half == 1)
                s_a = self.sem("silu_done", c2)
                with self.block() as block:
                    @block.scalar
                    def _(a):
                        nc.scalar.activation(U[:], U[:], ACT.Silu, scale=1.0 / D).then_inc(s_a, 1)
                self.linear(U, D, Wo[:], D, A)
                s_v = self.sem("dve_chain", c2)
                with self.block() as block:
                    @block.vector
                    def _(v):
                        w = Chain(v, s_v)
                        w(v.tensor_tensor(A[:], A[:], self.H[:], ALU.add))
                        w(v.tensor_tensor(self.X[:], self.X[:], A[:], ALU.add))

    def message_edges(self, Wm, NE_):
        nc = self.nc
        W = D + 1
        norm = (D * NE_) ** -0.5
        with ExitStack() as c:
            sb, sem = (lambda n, s, d=F32: self.sb(n, s, d, c)), (lambda n: self.sem(n, c))
            ST = [sb(f"start_values{b}", [P, CH, W]) for b in range(2)]
            EA = [sb(f"edge_attr{b}", [P, CH, NE_]) for b in range(2)]
            XF = [sb(f"dst_features{b}", [P, CH, D]) for b in range(2)]
            PM = [sb(f"outer{b}", [P, 4, D, NE_]) for b in range(2)]
            PT = [sb(f"outerT{b}", [P, 512]) for b in range(2)]
            D0 = sb("first_dst_rows", [P, W])
            o = self.scatter_buffers(c, False)
            srcc = sb("src_chunk", [P, CH])
            o.SRC = srcc
            tp = [self.ps(f"outerT_ps{b}", [P, 512], c) for b in range(2)]
            mp = [self.ps(f"message_ps{b}", [P, 512], c) for b in range(2)]
            s_in = [sem(f"inputs_in{b}") for b in range(2)]
            s_used, s_v, s_pm, s_t, s_pt, s_m, s_ms, o.s_src = (sem(x) for x in (
                "inputs_used", "dve_chain", "outer_ready", "transposed", "transposed_copied", "message_ready",
                "message_copied", "src_ready"))
            s_d0 = self.dsem("first_dst_in")
            GR = o.groups
            LAG = 3
            stv = self.starts17[0:E, :].rearrange("(p c) w -> p c w", p=P)
            eav = self.t["edge_attr_8"].rearrange("(p c) w -> p c w", p=P)
            with self.block() as block:
                @block.sync
                def _(sp):
                    def load(k, b):
                        at, used = held(sp, k * CH, k - 1)
                        if not first(k, 2):
                            sp.wait_ge(s_used, used)
                        sp.dma_start(ST[b][:], stv[:, ds(at, CH), :]).then_inc(s_in[b], 16)
                        sp.dma_start(EA[b][:], eav[:, ds(at, CH), :]).then_inc(s_in[b], 16)
                    chunks(sp, NCH, 3, load)

                @block.gpsimd
                def _(g):
                    g.indirect_dma_start(D0[:], None, self.tab17, bass.IndirectOffsetOnAxis(ap=self.dst0_i[:], axis=0)).then_inc(s_d0, 16)
                    chunks(g, NCH, 3, lambda k, b: self.scatter_pool(g, o, k, b))

                @block.tensor
                def _(pe):
                    def transposes(k, q):
                        n = min(4, CH - 4 * q)
                        pe.wait_ge(s_pm, k * GR + (q + 1))
                        if not first(k, 1) or q >= 2:
                            pe.wait_ge(s_pt, k * GR + (q - 1))
                        for j in range(n):
                            last = pe.transpose(tp[q % 2][:, j * P:(j + 1) * P], PM[q % 2][:, j].rearrange("p a b -> p (a b)"), self.ident[:])
                        last.then_inc(s_t, 1)

                    def src_rows(k, q):
                        n = min(4, CH - 4 * q)
                        if q == 0:
                            pe.wait_ge(o.s_src, k + 1)
                        if not first(k, 1) or q >= 2:
                            pe.wait_ge(o.s_eq, k * GR + (q - 1))
                        for j in range(n):
                            last = pe.matmul(o.row_ps[q % 2][:, j * P:(j + 1) * P], bcast(srcc[:, 4 * q + j:4 * q + j + 1], [P, P]),
                                             self.ident[:], start=True, stop=True)
                        last.then_inc(o.s_row, 1)

                    def sums(k, q):
                        n = min(4, CH - 4 * q)
                        pe.wait_ge(o.s_eq, k * GR + (q + 1))
                        pe.wait_ge(s_ms, k * GR + (q + 1))
                        if not first(k, 1) or q >= 1:
                            pe.wait_ge(o.s_sv, k * GR + q)
                        for j in range(n):
                            last = pe.matmul(o.sum_ps[:, q % 2, j * D:(j + 1) * D], o.EQ[q % o.nq][:, j, :], o.VAL[:, 4 * q + j, :],
                                             start=True, stop=True)
                        last.then_inc(o.s_sum, 1)

                    def products(k, b):
                        for s in range(GR + LAG):
                            if s < GR:
                                transposes(k, s)
                                src_rows(k, s)
                            if 1 <= s <= GR:
                                second(k, s - 1)
                            if s >= LAG:
                                sums(k, s - LAG)

                    def second(k, q):
                        n = min(4, CH - 4 * q)
                        pe.wait_ge(s_pt, k * GR + (q + 1))
                        if not first(k, 1) or q >= 2:
                            pe.wait_ge(s_ms, k * GR + (q - 1))
                        for j in range(n):
                            last = pe.matmul(mp[q % 2][:, j * D:(j + 1) * D], PT[q % 2][:, j * P:(j + 1) * P], Wm[:], start=True, stop=True)
                        last.then_inc(s_m, 1)
                    chunks(pe, NCH, 3, products)

                @block.scalar
                def _(a):
                    def silu(k, q):
                        n = min(4, CH - 4 * q)
                        a.wait_ge(s_m, k * GR + (q + 1))
                        if q == 0 and not first(k, 1):
                            a.wait_ge(o.s_sum, k * GR)
                        ins = nc.scalar.activation(o.VAL[:, 4 * q:4 * q + n, :], mp[q % 2][:, 0:n * D].rearrange("p (a b) -> p a b", b=D),
                                                   ACT.Silu, scale=norm)
                        ins.then_inc(s_ms, 1)

                    def sums_out(k, q, b):
                        n = min(4, CH - 4 * q)
                        if q == 0 and not first(k, 2):
                            a.wait_ge(o.s_chunk, k - 1)
                        a.wait_ge(o.s_sum, k * GR + (q + 1))
                        nc.scalar.activation(o.SV[b][:, 4 * q:4 * q + n, :], o.sum_ps[:, q % 2, 0:n * D].rearrange("p (a b) -> p a b", b=D),
                                             ACT.Copy).then_inc(o.s_sv, 1)

                    def step(k, b):
                        for s in range(GR + LAG):
                            if s < GR:
                                n = min(4, CH - 4 * s)
                                a.wait_ge(s_t, k * GR + (s + 1))
                                if not first(k, 1) or s >= 2:
                                    a.wait_ge(s_m, k * GR + (s - 1))
                                nc.scalar.activation(PT[s % 2][:, 0:n * P], tp[s % 2][:, 0:n * P], ACT.Copy).then_inc(s_pt, 1)
                            if 1 <= s <= GR:
                                silu(k, s - 1)
                            if s >= LAG:
                                sums_out(k, s - LAG, b)
                    chunks(a, NCH, 3, step)

                @block.vector
                def _(v):
                    w0 = Chain(v, s_v)
                    w0(v.memset(XF[1][:], 0.0))
                    K = [0]

                    def compute(k, b):
                        w = Chain(v, s_v, w0.n + k * K[0] if not first(k, 1) else w0.n)
                        sm = self.same[:, ds(k * CH, CH)]
                        m = k * 16 + 32 - 16 * b if not isinstance(k, int) else 32 * (k // 2 + 1)
                        v.wait_ge(s_in[b], m)
                        if first(k, 1):
                            v.wait_ge(s_d0, 16)
                            w(v.tensor_copy(ST[b][:, 0, :], D0[:]))
                        else:
                            v.wait_ge(o.s_sum, k * GR)
                            w(v.tensor_copy(srcc[:], self.srcf[:, ds(k * CH, CH)]))
                        if first(k, 1):
                            v.tensor_copy(srcc[:], self.srcf[:, ds(k * CH, CH)])
                        if not first(k, 2):
                            v.wait_ge(o.s_chunk, k - 1)
                        v.tensor_copy(o.IXS[b][:], self.sidx[:, ds(k * CH, CH)]).then_inc(o.s_ixs, 1)
                        for f in range(D):
                            ins = v.tensor_tensor_scan(XF[b][:, :, f], sm, ST[b][:, :, 1 + f], XF[1 - b][:, CH - 1, f:f + 1], ALU.mult, ALU.add)
                        w(ins)
                        v.sem_inc(o.s_src, 1)
                        for q in range(GR):
                            n = min(4, CH - 4 * q)
                            if not first(k, 1) or q >= 2:
                                v.wait_ge(s_t, k * GR + (q - 1))
                            v.tensor_tensor(PM[q % 2][:, 0:n], bcast(XF[b][:, 4 * q:4 * q + n, :].unsqueeze(3), [P, n, D, NE_]),
                                            bcast(EA[b][:, 4 * q:4 * q + n, :].unsqueeze(2), [P, n, D, NE_]), ALU.mult).then_inc(s_pm, 1)
                            v.wait_ge(o.s_row, k * GR + (q + 1))
                            if not first(k, 1) or q >= o.nq:
                                v.wait_ge(o.s_sum, k * GR + (q - o.nq + 1))
                            v.tensor_tensor(o.EQ[q % o.nq][:, 0:n, :], o.row_ps[q % 2][:, 0:n * P].rearrange("p (a b) -> p a b", b=P),
                                            bcast(srcc[:, 4 * q:4 * q + n].unsqueeze(2), [P, n, P]), ALU.is_equal).then_inc(o.s_eq, 1)
                        v.wait_ge(s_pm, k * GR + GR)
                        v.sem_inc(s_used, 1)
                        if first(k, 1):
                            K[0] = w.n
                        assert w.n == K[0]
                    chunks(v, NCH, 3, compute)

    def layer3(self):
        nc, t = self.nc, self.t
        with ExitStack() as c:
            sb = lambda n, s: self.sb(n, s, F32, c)
            self.qtab = self.dram("message_table", (NP, HID))
            self.hidden = self.dram("hidden", (NT // 2, P, 2 * 2 * P))
            rows = [self.dram(f"message_rows{h}", (E + 1, HID // 2)) for h in range(2)]
            b = {n: sb(n, [P, 2]) for n in ("pre_b1", "pre_b2", "post_b1")}
            rowb = {"conv_b": sb("conv_b", [1, HID]), "post_b2": sb("post_b2", [1, D])}
            ones = sb("ones", [1, P])
            pw2 = sb("post_w2", [P, 2, D])
            s_w, s_o = self.sem("weights_in", c), self.sem("ones_ready", c)
            halves = lambda ap: ap.rearrange("(k p) m -> p k m", p=P)
            with self.block() as block:
                @block.sync
                def _(sp):
                    loads = [(b[n][:], t[f"L3_gnn_{n}"].rearrange("(m p) -> p m", p=P)) for n in b]
                    loads += [(rowb[n][:], t[f"L3_gnn_{n}"].rearrange("(a n) -> a n", a=1)) for n in rowb]
                    loads.append((pw2[:], halves(t["L3_gnn_post_w2"])))
                    with nc.allow_non_contiguous_dma(reason="small biases, a value per partition"):
                        for dst, src in loads:
                            sp.dma_start(dst, src).then_inc(s_w, 16)
                    sp.wait_ge(s_w, 16 * len(loads))

                @block.vector
                def _(v):
                    v.memset(ones[:], 1.0).then_inc(s_o, 1)
            self.message_table(b, rowb, ones)
            self.message_sums(rows)
            self.output(b, rowb, ones, pw2, rows)

    def message_table(self, b, rowb, ones):
        nc, t = self.nc, self.t
        groups = NT // 2
        with ExitStack() as c:
            sb, sem, ps = (lambda n, s: self.sb(n, s, F32, c)), (lambda n: self.sem(n, c)), (lambda n: self.ps(n, [P, 2, 2 * P], c))
            w1 = sb("pre_w1", [D, HID])
            w2 = sb("pre_w2", [P, 2, HID])
            wc = sb("conv_w", [P, 2, HID])
            xs = [sb(f"staged{i}", [P, 2, D]) for i in range(2)]
            hT = sb("hT", [D, 2 * P])
            a1 = sb("hidden1", [P, 2, 2 * P])
            a2 = [sb(f"hidden2_{i}", [P, 2, 2 * P]) for i in range(2)]
            q = [sb(f"messages{i}", [P, 2, HID]) for i in range(2)]
            p0, p1, p2, p3 = (ps(f"ps{i}") for i in range(4))
            s_w, s_s, s_p, s_t, s_h, s_1, s_a1, s_2, s_a2, s_3, s_q = (sem(n) for n in (
                "weights_in", "staged", "pe_passed", "transposed", "hT_copied", "first_ready", "hidden1_ready", "second_ready",
                "hidden2_ready", "conv_ready", "messages_ready"))
            s_sp = sem("sp_passed")
            s_ho = [sem(f"hidden_out{i}") for i in range(2)]
            s_qo = [sem(f"messages_out{i}") for i in range(2)]
            halves = lambda ap: ap.rearrange("(k p) m -> p k m", p=P)
            tabv = self.qtab.rearrange("(p t) w -> p t w", p=P)
            hidv = self.hidden.rearrange("g p x -> p g x")
            with self.block() as block:
                @block.sync
                def _(sp):
                    for dst, src in ((w1[:], t["L3_gnn_pre_w1"]), (w2[:], halves(t["L3_gnn_pre_w2"])), (wc[:], halves(t["L3_gnn_conv_w"]))):
                        sp.dma_start(dst, src).then_inc(s_w, 16)

                    def store(g, i):
                        at, at2, n_a2, n_q = held(sp, g * 1, g * 2, 2 * g + 2, g + 1)
                        sp.wait_ge(s_a2, n_a2)
                        sp.sem_inc(s_sp, 1)
                        sp.dma_start(hidv[:, ds(at, 1), :], a2[i][:].rearrange("p m n -> p (m n)").unsqueeze(1)).then_inc(s_ho[i], 16)
                        sp.wait_ge(s_q, n_q)
                        sp.sem_inc(s_sp, 1)
                        sp.dma_start(tabv[:, ds(at2, 2), :], q[i][:]).then_inc(s_qo[i], 16)
                    chunks(sp, groups, 3, store)
                    for i in range(2):
                        n = (groups + 1 - i) // 2
                        sp.wait_ge(s_ho[i], 16 * n)
                        sp.wait_ge(s_qo[i], 16 * n)

                @block.gpsimd
                def _(pool):
                    def stage(g, i):
                        if not first(g, 2):
                            pool.wait_ge(s_t, g - 1)
                        pool.tensor_copy(xs[i][:], self.H[:, ds(g * 2, 2), :]).then_inc(s_s, 1)
                    chunks(pool, groups, 3, stage)

                @block.tensor
                def _(pe):
                    pe.wait_ge(s_w, 48)

                    def turn(g, i):
                        pe.wait_ge(s_s, g + 1)
                        if not first(g, 1):
                            pe.wait_ge(s_h, g)
                        pe.sem_inc(s_p, 1)
                        for j in range(2):
                            last = pe.transpose(p0[0:D, 0, j * P:(j + 1) * P], xs[i][:, j, :], self.ident[:])
                        last.then_inc(s_t, 1)

                    def one(g):
                        pe.wait_ge(s_h, g + 1)
                        if not first(g, 1):
                            pe.wait_ge(s_a1, 2 * g)
                        for m in range(2):
                            last = pe.matmul(p1[:, m, :], w1[:, m * P:(m + 1) * P], hT[:], start=True, stop=True)
                        last.then_inc(s_1, 1)

                    def product(g, i):
                        more = not (isinstance(g, int) and g == groups - 1)
                        if more:
                            turn(g + 1, 1 - i)
                        pe.wait_ge(s_a1, 2 * g + 2)
                        if not first(g, 1):
                            pe.wait_ge(s_a2, 2 * g)
                        for m in range(2):
                            for k in range(2):
                                last = pe.matmul(p2[:, m, :], w2[:, k, m * P:(m + 1) * P], a1[:, k, :], start=k == 0, stop=k == 1)
                        last.then_inc(s_2, 1)
                        if more:
                            one(g + 1)
                        pe.wait_ge(s_a2, 2 * g + 2)
                        if not first(g, 1):
                            pe.wait_ge(s_q, g)
                        for j in range(2):
                            for k in range(2):
                                pe.matmul(p3[:, j, :], a2[i][:, k, j * P:(j + 1) * P], wc[:, k, :], start=k == 0, stop=False)
                            last = pe.matmul(p3[:, j, :], ones[:], rowb["conv_b"][:], start=False, stop=True)
                        last.then_inc(s_3, 1)
                    turn(0, 0)
                    one(0)
                    chunks(pe, groups, 2, product, tail=1)

                @block.scalar
                def _(a):
                    def copy(g, i):
                        a.wait_ge(s_t, g + 1)
                        if not first(g, 1):
                            a.wait_ge(s_1, g)
                        nc.scalar.activation(hT[:], p0[0:D, 0, :], ACT.Copy).then_inc(s_h, 1)
                        a.wait_ge(s_1, g + 1)
                        if not first(g, 1):
                            a.wait_ge(s_2, g)
                        for m in range(2):
                            nc.scalar.activation(a1[:, m, :], p1[:, m, :], ACT.Relu, bias=b["pre_b1"][:, m:m + 1]).then_inc(s_a1, 1)
                    chunks(a, groups, 3, copy)

                @block.vector
                def _(v):
                    def evac(g, i):
                        v.wait_ge(s_2, g + 1)
                        if not first(g, 2):
                            v.wait_ge(s_ho[i], (g - i) * 8)
                            v.wait_ge(s_3, g - 1)
                        for m in range(2):
                            v.tensor_scalar(a2[i][:, m, :], p2[:, m, :], b["pre_b2"][:, m:m + 1], None, ALU.add).then_inc(s_a2, 1)
                        v.wait_ge(s_3, g + 1)
                        if not first(g, 2):
                            v.wait_ge(s_qo[i], (g - i) * 8)
                        v.tensor_scalar(q[i][:], p3[:], 0.0, None, ALU.max).then_inc(s_q, 1)
                    chunks(v, groups, 3, evac)

    def message_sums(self, rows):
        nc = self.nc
        RING = 4
        count = EP // SUB
        HALF = HID // 2
        with ExitStack() as c:
            sb, sem = (lambda n, s, d=F32: self.sb(n, s, d, c)), (lambda n: self.sem(n, c))
            IX = [sb(f"src_index{b}", [P, SUB], I32) for b in range(RING)]
            G = [sb(f"gathered{b}", [P, SUB, HID]) for b in range(RING)]
            SM = [sb(f"same{b}", [P, SUB]) for b in range(RING)]
            s_ix = [sem(f"index_in{b}") for b in range(RING)]
            s_o = [sem(f"rows_out{b}") for b in range(RING)]
            s_g = [self.dsem(f"gathered{b}") for b in range(RING)]
            s_v, s_done, s_pass, s_sp = sem("dve_chain"), sem("rows_ready"), sem("pool_passed"), sem("sp_passed")
            srcv = self.t["src"].rearrange("(p c) -> p c", p=P)
            outv = [r[0:E, :].rearrange("(p c) w -> p c w", p=P) for r in rows]
            peel = RING + count % RING
            turn = lambda k, b, per: (k // RING + 1) * per if isinstance(k, int) else k * (per // RING) + (per - b * (per // RING))
            with self.block() as block:
                @block.sync
                def _(sp):
                    def load(k, b):
                        at, stored, done = held(sp, k * SUB, turn(k, b, 32) - 32, k - (RING - 2))
                        if not first(k, RING):
                            sp.wait_ge(s_o[b], stored)
                            sp.sem_inc(s_sp, 1)
                            sp.wait_ge(s_done, done)
                            sp.sem_inc(s_sp, 1)
                        sp.dma_start(IX[b][:], srcv[:, ds(at, SUB)]).then_inc(s_ix[b], 16)
                    chunks(sp, count, peel, load, RING)

                @block.gpsimd
                def _(g):
                    def gather(k, b):
                        g.wait_ge(s_ix[b], turn(k, b, 16))
                        g.sem_inc(s_pass, 1)
                        for j in range(SUB):
                            g.indirect_dma_start(G[b][:, j, :], None, self.qtab, bass.IndirectOffsetOnAxis(
                                ap=IX[b][:, j:j + 1], axis=0)).then_inc(s_g[b], 16)
                    chunks(g, count, peel, gather, RING)

                @block.vector
                def _(v):
                    def scan(k, b):
                        v.wait_ge(s_g[b], turn(k, b, 16 * SUB))
                        base = k * (2 * SUB + 1)
                        if not first(k, 1):
                            v.wait_ge(s_v, base)
                        v.tensor_copy(SM[b][:], self.same[:, ds(k * SUB, SUB)]).then_inc(s_v, 1)
                        for j in range(SUB):
                            for h in range(2):
                                cut = slice(h * HALF, (h + 1) * HALF)
                                before = G[b][:, j - 1, cut] if j else G[(b - 1) % RING][:, SUB - 1, cut]
                                if first(k, 1) and j == 0:
                                    v.tensor_copy(G[b][:, 0, cut], G[b][:, 0, cut]).then_inc(s_v, 1)
                                    continue
                                v.wait_ge(s_v, base + (2 * j + h if j else 1))
                                v.scalar_tensor_tensor(G[b][:, j, cut], before, SM[b][:, j:j + 1], G[b][:, j, cut],
                                                       ALU.mult, ALU.add).then_inc(s_v, 1)
                        v.wait_ge(s_v, base + (2 * SUB + 1))
                        v.sem_inc(s_done, 1)
                    chunks(v, count, peel, scan, RING)
                    v.tensor_copy(self.tail[:], G[(count - 1) % RING][:, SUB - 1, :])

                @block.scalar
                def _(a):
                    def store(k, b):
                        at = k * SUB if isinstance(k, int) else a.snap(k * SUB)
                        a.wait_ge(s_done, k + 1)
                        for h in range(2):
                            a.dma_start(outv[h][:, ds(at, SUB), :], G[b][:, :, h * HALF:(h + 1) * HALF]).then_inc(s_o[b], 16)
                    chunks(a, count, peel, store, RING)
                    for b in range(RING):
                        a.wait_ge(s_o[b], 32 * ((count - b + RING - 1) // RING))
        for h in range(2):
            self.fixup(rows[h], HALF, self.tail[:, h * HALF:(h + 1) * HALF])

    def output(self, b, rowb, ones, pw2, rows):
        nc, t = self.nc, self.t
        groups = NT // 2
        with ExitStack() as c:
            sb, sem, ps = (lambda n, s, d=F32: self.sb(n, s, d, c)), (lambda n: self.sem(n, c)), (lambda n: self.ps(n, [P, 2, 2 * P], c))
            w1 = sb("post_w1", [P, 4, HID])
            EI = [sb(f"end_index{i}", [P, 2], I32) for i in range(2)]
            AG = [sb(f"sums{i}", [P, 2, HID]) for i in range(2)]
            HD = [sb(f"hidden{i}", [P, 2, 2 * P]) for i in range(2)]
            aT = sb("sumsT", [P, 2, 2 * P])
            z = sb("hidden3", [P, 2, 2 * P])
            th = [sb(f"tanh{i}", [P, 2, D]) for i in range(2)]
            p0, p1, p2 = (ps(f"ps{i}") for i in range(3))
            s_w, s_ei, s_t, s_aT, s_1, s_z, s_2, s_th, s_x, s_out, s_p = (sem(n) for n in (
                "weights_in", "end_index_staged", "transposed", "sumsT_copied", "hidden_ready", "hidden3_ready", "output_ready",
                "tanh_done", "residual_done", "output_out", "passed"))
            s_sp = sem("sp_passed")
            s_hd = [sem(f"hidden_in{i}") for i in range(2)]
            s_g = [self.dsem(f"sums_in{i}") for i in range(2)]
            hidv = self.hidden.rearrange("g p x -> p g x")
            with self.block() as block:
                @block.sync
                def _(sp):
                    sp.dma_start(w1[:], t["L3_gnn_post_w1"].rearrange("(k p) m -> p k m", p=P)).then_inc(s_w, 16)

                    def load(g, i):
                        at, used = held(sp, g * 1, g - 1)
                        if not first(g, 2):
                            sp.wait_ge(s_1, used)
                            sp.sem_inc(s_sp, 1)
                        sp.dma_start(HD[i][:].rearrange("p m n -> p (m n)").unsqueeze(1), hidv[:, ds(at, 1), :]).then_inc(s_hd[i], 16)
                    chunks(sp, groups, 3, load)
                    sp.wait_ge(s_x, groups)
                    sp.dma_start(self.out[0:FULL * NT, :].rearrange("(p t) d -> p t d", t=NT), self.X[0:FULL, :, :]).then_inc(s_out, 16)
                    sp.dma_start(self.out[FULL * NT:N, :].rearrange("(p t) d -> p t d", p=1), self.X[FULL:FULL + 1, 0:REST, :]).then_inc(s_out, 16)
                    sp.wait_ge(s_out, 32)

                @block.gpsimd
                def _(pool):
                    def gather(g, i):
                        if not first(g, 2):
                            pool.wait_ge(s_t, g - 1)
                            pool.wait_ge(s_g[i], (g - i) * 32)
                        pool.tensor_copy(EI[i][:], self.end_i[:, ds(g * 2, 2)]).then_inc(s_ei, 1)
                        pool.wait_ge(s_ei, g + 1)
                        pool.sem_inc(s_p, 1)
                        for j in range(2):
                            for h in range(2):
                                pool.indirect_dma_start(AG[i][:, j, h * P:(h + 1) * P], None, rows[h], bass.IndirectOffsetOnAxis(
                                    ap=EI[i][:, j:j + 1], axis=0)).then_inc(s_g[i], 16)
                    chunks(pool, groups, 3, gather)

                @block.tensor
                def _(pe):
                    pe.wait_ge(s_w, 16)

                    def turn(g, i):
                        pe.wait_ge(s_g[i], (g - i) * 32 + 64)
                        if not first(g, 1):
                            pe.wait_ge(s_aT, g)
                        for h in range(2):
                            for j in range(2):
                                last = pe.transpose(p0[:, h, j * P:(j + 1) * P], AG[i][:, j, h * P:(h + 1) * P], self.ident[:])
                        last.then_inc(s_t, 1)

                    def product(g, i):
                        pe.wait_ge(s_aT, g + 1)
                        pe.wait_ge(s_hd[i], (g - i) * 8 + 16)
                        if not first(g, 1):
                            pe.wait_ge(s_z, 2 * g)
                        for m in range(2):
                            for k in range(4):
                                src = HD[i][:, k, :] if k < 2 else aT[:, k - 2, :]
                                last = pe.matmul(p1[:, m, :], w1[:, k, m * P:(m + 1) * P], src, start=k == 0, stop=k == 3)
                        last.then_inc(s_1, 1)
                        if not (isinstance(g, int) and g == groups - 1):
                            turn(g + 1, 1 - i)
                        pe.wait_ge(s_z, 2 * g + 2)
                        if not first(g, 1):
                            pe.wait_ge(s_th, g)
                        for j in range(2):
                            for k in range(2):
                                pe.matmul(p2[:, 0, j * D:(j + 1) * D], z[:, k, j * P:(j + 1) * P], pw2[:, k, :], start=k == 0, stop=False)
                            last = pe.matmul(p2[:, 0, j * D:(j + 1) * D], ones[:], rowb["post_b2"][:], start=False, stop=True)
                        last.then_inc(s_2, 1)
                    turn(0, 0)
                    chunks(pe, groups, 2, product, tail=1)

                @block.scalar
                def _(a):
                    def copy(g):
                        a.wait_ge(s_t, g + 1)
                        if not first(g, 1):
                            a.wait_ge(s_1, g)
                        nc.scalar.activation(aT[:], p0[:], ACT.Copy).then_inc(s_aT, 1)

                    def act(g, i):
                        a.wait_ge(s_1, g + 1)
                        if not first(g, 1):
                            a.wait_ge(s_2, g)
                        for m in range(2):
                            nc.scalar.activation(z[:, m, :], p1[:, m, :], ACT.Relu, bias=b["post_b1"][:, m:m + 1]).then_inc(s_z, 1)
                        if not (isinstance(g, int) and g == groups - 1):
                            copy(g + 1)
                        a.wait_ge(s_2, g + 1)
                        if not first(g, 2):
                            a.wait_ge(s_x, g - 1)
                        nc.scalar.activation(th[i][:], p2[:, 0, 0:2 * D].rearrange("p (a b) -> p a b", b=D), ACT.Tanh).then_inc(s_th, 1)
                    copy(0)
                    chunks(a, groups, 2, act, tail=1)

                @block.vector
                def _(v):
                    def add(g, i):
                        v.wait_ge(s_th, g + 1)
                        x = self.X[:, ds(g * 2, 2), :]
                        v.tensor_tensor(x, x, th[i][:], ALU.add).then_inc(s_x, 1)
                    chunks(v, groups, 3, add)


def four_layers(nc, t, out):
    with ExitStack() as ctx:
        k = Kernel(nc, ctx, t, out)
        k.setup()
        for layer in (k.layer0, k.layer1, k.layer2, k.layer3):
            k.layer_norm()
            layer()


_INS = ['x', 'src', 'dst', 'edge_attr_8', 'L0_gnn_W1', 'L0_gnn_a_src1', 'L0_gnn_a_dst1', 'L0_gnn_b1', 'L0_gnn_W2',
        'L0_gnn_a_src2', 'L0_gnn_a_dst2', 'L0_gnn_b2', 'L0_gnn_Wf', 'L0_gnn_bf', 'L1_gnn_W1', 'L1_gnn_b1', 'L1_gnn_W2',
        'L1_gnn_b2', 'L2_gnn_W_msg_tp', 'L2_gnn_W_msg_lin', 'L2_gnn_W_upd_tp', 'L2_gnn_W_upd_lin', 'L3_gnn_pre_w1',
        'L3_gnn_pre_b1', 'L3_gnn_pre_w2', 'L3_gnn_pre_b2', 'L3_gnn_conv_w', 'L3_gnn_conv_b', 'L3_gnn_post_w1',
        'L3_gnn_post_b1', 'L3_gnn_post_w2', 'L3_gnn_post_b2']


def kernel(**inputs):
    import numpy as _np
    import concourse.bacc as _bacc
    from concourse import mybir as _mybir
    from concourse.bass_utils import run_bass_kernel_spmd as _run

    nc = _bacc.Bacc("TRN2", target_bir_lowering=False, num_devices=1)
    arrays, args = {}, {}
    for name in _INS:
        a = _np.ascontiguousarray(inputs[name])
        arrays[f"in_{name}_dram"] = a
        args[name] = nc.dram_tensor(f"in_{name}_dram", a.shape, _mybir.dt.from_np(a.dtype), kind="ExternalInput").ap()
    out = nc.dram_tensor("out_0_dram", (N, D), _mybir.dt.float32, kind="ExternalOutput").ap()
    four_layers(nc, args, out)
    r = _run(nc, [arrays], core_ids=[0])
    return r.results[0]["out_0_dram"]
```
